# Optimizing a Trainium2 kernel written in Bass

```python
import numpy as np
import jax
import jax.numpy as jnp

def _softmax(x, axis=-1):
    return jax.nn.softmax(x, axis=axis)
def _gelu(x):
    return jax.nn.gelu(x, approximate=True)
def _silu(x):
    return jax.nn.silu(x)
def _sigmoid(x):
    return jax.nn.sigmoid(x)
def _layernorm(x, axis=-1, eps=1e-5):
    m = jnp.mean(x, axis=axis, keepdims=True)
    v = jnp.var(x, axis=axis, keepdims=True)
    return (x - m) / jnp.sqrt(v + eps)
def _scatter_add(tgt, idx, src, axis=0):
    return tgt.at[idx].add(src)
def _segment_sum(src, seg, n):
    return jax.ops.segment_sum(src, seg, n)

kernel_name = 'mk_conv_seq_d1_conv_nhwc96_23ea7d'

def setup_inputs(seed: int = 0):
    np.random.seed(seed)
    _w = jnp.asarray
    def _rec_inputs():
        import jax
        import jax.numpy as jnp
        _gk = jax.random.key(seed)
        x = -0.0002221 + 1 * jax.random.normal(jax.random.fold_in(_gk, 1), (4, 256, 256, 96), jnp.float32)
        return x
    x = _rec_inputs()
    def _L0_conv_setup():
        import jax, jax.numpy as jnp
        import numpy as np
        EMBED = 96
        HEADS = 3
        KD = EMBED // HEADS
        WIN = 8
        SHIFT = 4
        EPS = 1e-06

        def _ln(x, g, b):
            m = jnp.mean(x, axis=-1, keepdims=True)
            v = jnp.mean(jnp.square(x - m), axis=-1, keepdims=True)
            return (x - m) * jax.lax.rsqrt(v + EPS) * g + b
        key = jax.random.key(seed)
        ks = jax.random.split(key, 8)
        d = EMBED
        s = 0.02

        def rn(k, shape):
            return jax.random.normal(k, shape, jnp.float32) * s
        return {'x': jax.random.normal(ks[0], (4, 256, 256, d), jnp.float32), 'ln1_g': jnp.ones((d,), jnp.float32), 'ln1_b': jnp.zeros((d,), jnp.float32), 'wq': rn(ks[1], (d, HEADS, KD)), 'bq': jnp.zeros((HEADS, KD), jnp.float32), 'wk': rn(ks[2], (d, HEADS, KD)), 'bk': jnp.zeros((HEADS, KD), jnp.float32), 'wv': rn(ks[3], (d, HEADS, KD)), 'bv': jnp.zeros((HEADS, KD), jnp.float32), 'wo': rn(ks[4], (HEADS, KD, d)), 'bo': jnp.zeros((d,), jnp.float32), 'ln2_g': jnp.ones((d,), jnp.float32), 'ln2_b': jnp.zeros((d,), jnp.float32), 'w1': rn(ks[5], (d, 4 * d)), 'b1': jnp.zeros((4 * d,), jnp.float32), 'w2': rn(ks[6], (4 * d, d)), 'b2': jnp.zeros((d,), jnp.float32)}
    _L0_conv_all = _L0_conv_setup()
    _L0_conv_in = {k: v for k, v in _L0_conv_all.items() if k in ('ln1_g', 'ln1_b', 'wq', 'bq', 'wk', 'bk', 'wv', 'bv', 'wo', 'bo', 'ln2_g', 'ln2_b', 'w1', 'b1', 'w2', 'b2', )}
    del _L0_conv_all

    return {
        "x": x,
        "L0_conv_ln1_g": _L0_conv_in["ln1_g"],
        "L0_conv_ln1_b": _L0_conv_in["ln1_b"],
        "L0_conv_wq": _L0_conv_in["wq"],
        "L0_conv_bq": _L0_conv_in["bq"],
        "L0_conv_wk": _L0_conv_in["wk"],
        "L0_conv_bk": _L0_conv_in["bk"],
        "L0_conv_wv": _L0_conv_in["wv"],
        "L0_conv_bv": _L0_conv_in["bv"],
        "L0_conv_wo": _L0_conv_in["wo"],
        "L0_conv_bo": _L0_conv_in["bo"],
        "L0_conv_ln2_g": _L0_conv_in["ln2_g"],
        "L0_conv_ln2_b": _L0_conv_in["ln2_b"],
        "L0_conv_w1": _L0_conv_in["w1"],
        "L0_conv_b1": _L0_conv_in["b1"],
        "L0_conv_w2": _L0_conv_in["w2"],
        "L0_conv_b2": _L0_conv_in["b2"],
    }

def reference(x, L0_conv_ln1_g, L0_conv_ln1_b, L0_conv_wq, L0_conv_bq, L0_conv_wk, L0_conv_bk, L0_conv_wv, L0_conv_bv, L0_conv_wo, L0_conv_bo, L0_conv_ln2_g, L0_conv_ln2_b, L0_conv_w1, L0_conv_b1, L0_conv_w2, L0_conv_b2):
    import jax
    import jax.numpy as jnp
    def _L0_conv_ref(x, ln1_g, ln1_b, wq, bq, wk, bk, wv, bv, wo, bo, ln2_g, ln2_b, w1, b1, w2, b2):
        import jax, jax.numpy as jnp
        import numpy as np
        EMBED = 96
        HEADS = 3
        KD = EMBED // HEADS
        WIN = 8
        SHIFT = 4
        EPS = 1e-06

        def _ln(x, g, b):
            m = jnp.mean(x, axis=-1, keepdims=True)
            v = jnp.mean(jnp.square(x - m), axis=-1, keepdims=True)
            return (x - m) * jax.lax.rsqrt(v + EPS) * g + b
        B, H, W, C = x.shape
        xs = jnp.roll(x, shift=(-SHIFT, -SHIFT), axis=(1, 2))
        win = xs.reshape(B, H // WIN, WIN, W // WIN, WIN, C)
        win = win.transpose(0, 1, 3, 2, 4, 5).reshape(-1, WIN * WIN, C)
        h = _ln(win, ln1_g, ln1_b)
        q = jnp.einsum('ntc,chd->nthd', h, wq) + bq
        k = jnp.einsum('ntc,chd->nthd', h, wk) + bk
        v = jnp.einsum('ntc,chd->nthd', h, wv) + bv
        scores = jnp.einsum('nqhd,nkhd->nhqk', q, k) * (1.0 / np.sqrt(KD))
        attn = jax.nn.softmax(scores, axis=-1)
        o = jnp.einsum('nhqk,nkhd->nqhd', attn, v)
        attn_out = jnp.einsum('nqhd,hdc->nqc', o, wo) + bo
        win = win + attn_out
        h2 = _ln(win, ln2_g, ln2_b)
        mlp = jax.nn.gelu(h2 @ w1 + b1, approximate=False) @ w2 + b2
        win = win + mlp
        x2 = win.reshape(B, H // WIN, W // WIN, WIN, WIN, C)
        x2 = x2.transpose(0, 1, 3, 2, 4, 5).reshape(B, H, W, C)
        return jnp.roll(x2, shift=(SHIFT, SHIFT), axis=(1, 2))

    def _gn(v, G=32, eps=1e-5):
        B_, H_, W_, C_ = v.shape
        g = v.reshape(B_, H_, W_, G, C_ // G)
        m = jnp.mean(g, axis=(1, 2, 4), keepdims=True)
        s = jnp.var(g, axis=(1, 2, 4), keepdims=True)
        return ((g - m) / jnp.sqrt(s + eps)).reshape(v.shape)

    def _ln_c(v, eps=1e-6):
        m = jnp.mean(v, axis=-1, keepdims=True)
        s = jnp.var(v, axis=-1, keepdims=True)
        return (v - m) / jnp.sqrt(s + eps)

    def _ln_t(v, eps=1e-5):
        m = jnp.mean(v, axis=-1, keepdims=True)
        s = jnp.var(v, axis=-1, keepdims=True)
        return (v - m) / jnp.sqrt(s + eps)

    def _to_tokens(v):
        B_, H_, W_, C_ = v.shape
        return v.reshape(B_, H_ * W_, C_)
    def _from_tokens(t, like):
        return t.reshape(like.shape)

    x = _L0_conv_ref(x, L0_conv_ln1_g, L0_conv_ln1_b, L0_conv_wq, L0_conv_bq, L0_conv_wk, L0_conv_bk, L0_conv_wv, L0_conv_bv, L0_conv_wo, L0_conv_bo, L0_conv_ln2_g, L0_conv_ln2_b, L0_conv_w1, L0_conv_b1, L0_conv_w2, L0_conv_b2)
    return x


_drawn_inputs = setup_inputs


def setup_inputs(seed=0):
    import zlib

    import numpy as np

    out = dict(_drawn_inputs(seed))
    spreads = {'L0_conv_ln1_g': (1.0, 0.6),
     'L0_conv_ln1_b': (0.0, 0.8),
     'L0_conv_bq': (0.0, 0.8),
     'L0_conv_bk': (0.0, 0.8),
     'L0_conv_bv': (0.0, 0.372),
     'L0_conv_bo': (0.0, 0.1),
     'L0_conv_ln2_g': (1.0, 0.6),
     'L0_conv_ln2_b': (0.0, 0.8),
     'L0_conv_b1': (0.0, 0.423),
     'L0_conv_b2': (0.0, 0.1)}
    factors = {'L0_conv_wq': 8.0, 'L0_conv_wk': 8.0, 'L0_conv_wv': 8.0}
    for name, (base, spread) in spreads.items():
        noise = np.random.default_rng([zlib.crc32(name.encode()), seed]).standard_normal(out[name].shape)
        drawn = base * np.exp(spread * noise) if base else spread * noise
        out[name] = jnp.asarray(drawn.astype(out[name].dtype))
    for name, factor in factors.items():
        out[name] = (out[name] * factor).astype(out[name].dtype)
    return out
```

```python
from contextlib import ExitStack

import concourse.bass as bass
from concourse import mybir

FP32 = mybir.dt.float32
ALU = mybir.AluOpType
ACT = mybir.ActivationFunctionType
AXIS = mybir.AxisListType

IMAGES, HEIGHT, WIDTH, C = 4, 256, 256, 96
HEADS, KD, WIN, SHIFT = 3, 32, 8, 4
F = 4 * C
FCHUNKS = F // 128
EPS = 1e-6
SCALE = KD ** -0.5
P = 128

WROWS = IMAGES * HEIGHT // WIN
UNITS = 2 * WROWS
WINDOWS = WIDTH // WIN // 2
WT = WIN * WIN
TOK = WINDOWS * WT
TILES = TOK // P
QUADS = WINDOWS // 4
BATCH = 16
BATCH_ROWS = BATCH // 2
BATCHES = UNITS // BATCH
SLOTS = 2 * BATCH
ROW = WIDTH * C
SEG = WIN * C
ONES = C
LOAD_DMAS = (2, 6)
SHARES = TOK // 2
SCORES, GROUP = 8 * WT, 4 * C


def swin_block(nc, x, ln1_g, ln1_b, wq, bq, wk, bk, wv, bv, wo, bo, ln2_g, ln2_b, w1, b1, w2, b2, out):
    x_rows = x.rearrange("b (g r) w c -> (b g) r (w c)", r=SHIFT)
    out_rows = out.rearrange("b (g r) w c -> (b g) r (w c)", r=SHIFT)

    with ExitStack() as ctx:
        def sb(name, *shape):
            return ctx.enter_context(nc.sbuf_tensor(name, list(shape), FP32))

        def sem(name):
            return ctx.enter_context(nc.semaphore(name))

        stream = sb("stream", P, SLOTS, SEG)
        normed = sb("normed", P, TILES, C)
        hT = sb("hT", P, TOK)
        qT = sb("qT", C, TOK)
        kT = sb("kT", C, TOK)
        v = sb("v", P, QUADS, 2, C)
        probs = sb("probs", P, QUADS, HEADS, 2, WT)
        probsT = sb("probsT", P, HEADS, QUADS, P)
        oT = sb("oT", P, TOK)
        h2T = sb("h2T", P, TOK)
        gelu = sb("gelu", P, FCHUNKS, TOK)
        qkv_raw = sb("qkv_raw", C, 3, C)
        qkv_w = sb("qkv_w", P, 3, C)
        wo_w = sb("wo_w", P, C)
        w1_raw = sb("w1_raw", C, F)
        w1_w = sb("w1_w", P, F)
        w2_w = sb("w2_w", P, FCHUNKS, C)
        b2_all = sb("b2_all", P, C)
        ln_cols = sb("ln_cols", C, 4)
        bias_rows = sb("bias_rows", P, 3 * C + F)
        ident = sb("ident", P, P)
        eps_col = sb("eps_col", P, 1)
        stats = [sb(f"stats{i}", P, TILES, 6) for i in (1, 2)]
        mean_sum = [sb(f"mean_sum{i}", P, TILES) for i in (1, 2)]
        mean_gap = [sb(f"mean_gap{i}", P, TILES) for i in (1, 2)]
        within = [sb(f"within{i}", P, TILES) for i in (1, 2)]
        between = [sb(f"between{i}", P, TILES) for i in (1, 2)]
        sq_dev = [sb(f"sq_dev{i}", P, TILES) for i in (1, 2)]
        log_var = [sb(f"log_var{i}", P, TILES) for i in (1, 2)]
        mean1 = sb("mean1", P, TILES)
        rstd1 = sb("rstd1", P, TILES)
        mean2 = sb("mean2", P, BATCH, TILES)
        rstd2 = sb("rstd2", P, BATCH, TILES)
        mean2_now = sb("mean2_now", P, TILES)
        rstd2_now = sb("rstd2_now", P, TILES)
        neg_max = sb("neg_max", P, HEADS, 2 * QUADS)
        exp_bias = sb("exp_bias", P, HEADS, 2 * QUADS)
        prob_sum = sb("prob_sum", P, HEADS, 2 * QUADS)
        prob_inv = sb("prob_inv", P, HEADS, 2 * QUADS)

        psum = ctx.enter_context(nc.psum_tensor("psum", [P, 8, 512], FP32))
        S_BANKS = (0, 1, 2)
        PT_BANKS = (3, 4, 5)
        PV_BANKS = (6, 7)
        V_BANKS = (3, 4)
        T_BANKS = (5, 6)
        O_BANKS = (7, 3)
        QK_BANKS = (4, 5, 6, 7)
        T2_BANKS = (0, 1)
        UP_BANKS = ((0, 2, 1), (3, 4, 5))
        DOWN_BANKS = (6, 7)

        weights_in = sem("weights_in")
        consts_set = sem("consts_set")
        passed = sem("passed")
        ident_zeroed = sem("ident_zeroed")
        rows_cleared = sem("rows_cleared")
        bias_folded = sem("bias_folded")
        weights_ready = sem("weights_ready")
        x_loaded = [sem("x_loaded_left"), sem("x_loaded_right")]
        stored = sem("stored")
        ln1_step = sem("ln1_step")
        ln2_step = sem("ln2_step")
        max_step = sem("max_step")
        copy_step = sem("copy_step")
        log1_step = sem("log1_step")
        log2_step = sem("log2_step")
        rstd1_ready = sem("rstd1_ready")
        ln1_ready = sem("ln1_ready")
        t1_done = sem("t1_done")
        hT_copied = sem("hT_copied")
        qk_done = sem("qk_done")
        qk_copied = sem("qk_copied")
        v_done = sem("v_done")
        v_copied = sem("v_copied")
        scores_done = sem("scores_done")
        bias_ready = sem("bias_ready")
        exp_done = sem("exp_done")
        inv_ready = sem("inv_ready")
        probs_ready = sem("probs_ready")
        pt_done = sem("pt_done")
        pt_copied = sem("pt_copied")
        pv_done = sem("pv_done")
        oT_copied = sem("oT_copied")
        o_done = sem("o_done")
        attn_added = sem("attn_added")
        sq2_ready = sem("sq2_ready")
        rstd2_ready = sem("rstd2_ready")
        ln2_ready = sem("ln2_ready")
        b2_added = sem("b2_added")
        t2_done = sem("t2_done")
        h2T_copied = sem("h2T_copied")
        up_done = sem("up_done")
        gelu_done = sem("gelu_done")
        down_done = sem("down_done")
        mlp_added = sem("mlp_added")

        N_WEIGHT_DMAS = 15
        LN_STEPS = 6

        block = ctx.enter_context(nc.Block())

        def wait_apart(eng, semaphore, count):
            eng.wait_ge(semaphore, count)
            eng.sem_inc(passed, 1)

        def pieces(row, half):
            upper = 2 * row + 1
            if isinstance(row, int):
                lower = 2 * ((row // 32) * 32 + (row + 1) % 32)
            else:
                lower = 2 * ((row & (WROWS - 32)) + ((row + 1) & 31))
            for part, group in ((0, upper), (1, lower)):
                first = 64 * part
                if half == 0:
                    yield group, SHIFT * C, first, WINDOWS, SEG, 0
                else:
                    yield group, SHIFT * C + WINDOWS * SEG, first, WINDOWS - 1, SEG, 0
                    edge = first + 4 * (WINDOWS - 1)
                    yield group, ROW - SHIFT * C, edge, 1, SHIFT * C, 0
                    yield group, 0, edge, 1, SHIFT * C, SHIFT * C

        def dram_and_sbuf(rows, row, half, slot):
            for group, col, first, n, width, at in pieces(row, half):
                dram = rows[group, :, col:col + n * width].rearrange("r (w e) -> w r e", e=width)
                yield dram, stream[first:first + 4 * n, slot, at:at + width]

        @block.sync
        def _(sp):
            for i, w in enumerate((wq, wk, wv)):
                sp.dma_start(qkv_raw[:, i, :], w.rearrange("c h d -> c (h d)")).then_inc(weights_in, 16)
            for i, b in enumerate((bq, bk, bv)):
                sp.dma_start(bias_rows[ONES:ONES + 1, i * C:(i + 1) * C],
                             b.rearrange("(a h) d -> a (h d)", a=1)).then_inc(weights_in, 16)
            sp.dma_start(bias_rows[ONES:ONES + 1, 3 * C:3 * C + F],
                         b1.rearrange("(a n) -> a n", a=1)).then_inc(weights_in, 16)
            sp.dma_start(w1_raw[:, :], w1).then_inc(weights_in, 16)
            for i, col in enumerate((ln1_g, ln1_b, ln2_g, ln2_b)):
                sp.dma_start(ln_cols[:, i:i + 1], col.rearrange("(c a) -> c a", a=1)).then_inc(weights_in, 16)
            sp.dma_start(w2_w[:, :, :], w2.rearrange("(j p) c -> p j c", p=P)).then_inc(weights_in, 16)
            sp.dma_start(b2_all[:, :], b2.partition_broadcast(P)).then_inc(weights_in, 16)
            sp.dma_start(wo_w[0:C, :], wo.rearrange("h d c -> (h d) c")).then_inc(weights_in, 16)

            def load(row, source_row, half):
                if not (isinstance(row, int) and row == 0):
                    wait_apart(sp, x_loaded[half], 16 * LOAD_DMAS[half] * row)
                slot = (2 * row + half) % SLOTS if isinstance(row, int) else (2 * row + half) & (SLOTS - 1)
                for dram, sbuf in dram_and_sbuf(x_rows, source_row, half, slot):
                    sp.dma_start(sbuf, dram).then_inc(x_loaded[half], 16)

            def store(row, half):
                wait_apart(sp, mlp_added, 2 * (2 * row + half + 1))
                slot = (2 * row + half) & (SLOTS - 1)
                for dram, sbuf in dram_and_sbuf(out_rows, row, half, slot):
                    sp.dma_start(dram, sbuf).then_inc(stored, 16)

            def store_batch(batch_row):
                with sp.Fori(0, BATCH_ROWS) as r:
                    for half in (0, 1):
                        store(batch_row + r, half)
                wait_apart(sp, stored, 16 * sum(LOAD_DMAS) * (batch_row + BATCH_ROWS))

            for half in (0, 1):
                load(0, 0, half)
            with sp.Fori(1, 2 * BATCH_ROWS) as row:
                for half in (0, 1):
                    load(row, row, half)
            with sp.Fori(0, BATCHES - 2) as b:
                store_batch(b * BATCH_ROWS)
                with sp.Fori(0, BATCH_ROWS) as r:
                    for half in (0, 1):
                        row = b * BATCH_ROWS + r + 2 * BATCH_ROWS
                        load(row, row, half)
            store_batch(WROWS - 2 * BATCH_ROWS)
            for half in (0, 1):
                load(WROWS, 0, half)
            store_batch(WROWS - BATCH_ROWS)

        @block.gpsimd
        def _(pool):
            nc.gpsimd.memset(ident[:, :], 0.0).then_inc(ident_zeroed, 1)
            pool.wait_ge(ident_zeroed, 1)
            nc.gpsimd.affine_select(out=ident[:, :], in_=ident[:, :], compare_op=ALU.not_equal, fill=1.0,
                                    base=0, pattern=[[-1, P]], channel_multiplier=1).then_inc(consts_set, 1)

            def normalise_probs(u):
                pool.wait_ge(inv_ready, u + 1)
                for h in range(HEADS):
                    block_h = probs[:, :, h, :, :]
                    inv = prob_inv[:, h, :].rearrange("p (q a) -> p q a", a=2).unsqueeze(3)\
                        .to_broadcast((P, QUADS, 2, WT))
                    nc.gpsimd.tensor_tensor(block_h, block_h, inv, ALU.mult).then_inc(probs_ready, 1)

            def add_b2(u):
                pool.wait_ge(ln2_ready, u + 1)
                now = stream[:, u & (SLOTS - 1), :].rearrange("p (t c) -> p t c", c=C)
                nc.gpsimd.tensor_tensor(now, now, b2_all[:, :].unsqueeze(1).to_broadcast((P, TILES, C)),
                                        ALU.add).then_inc(b2_added, 1)

            pool.wait_ge(weights_in, 16 * (N_WEIGHT_DMAS + 1))
            normalise_probs(0)
            with pool.Fori(0, BATCHES) as b:
                batch = b * BATCH
                with pool.Fori(0, BATCH) as j:
                    normalise_probs(batch + j + 1)
                with pool.Fori(0, BATCH) as j:
                    add_b2(batch + j)

        @block.tensor
        def _(pe):
            pe.wait_ge(weights_in, 16 * (N_WEIGHT_DMAS + 1))
            nc.tensor.matmul(psum[ONES:ONES + 1, 0, 0:3 * C], ln_cols[:, 1:2],
                             qkv_raw[:, :, :].rearrange("c i n -> c (i n)"), start=True, stop=True)
            nc.tensor.matmul(psum[ONES:ONES + 1, 1, 0:F], ln_cols[:, 3:4], w1_raw[:, :],
                             start=True, stop=True).then_inc(bias_folded, 1)
            pe.wait_ge(weights_ready, 4)
            pe.wait_ge(consts_set, 5)

            def transpose_rows(banks, done, bank_free=None):
                for c in range(TILES):
                    if c == 4 and bank_free is not None:
                        pe.wait_ge(*bank_free)
                    last = nc.tensor.transpose(psum[0:C, banks[c // 4], (c % 4) * P:(c % 4 + 1) * P],
                                               normed[:, c, :], ident[:, :])
                    if c % 4 == 3:
                        last.then_inc(done, 1)

            def transpose1(u, steady):
                pe.wait_ge(ln1_ready, u + 1)
                transpose_rows(T_BANKS, t1_done, (oT_copied, 2 * u - 3) if steady else None)

            def project_qk(u, steady):
                pe.wait_ge(hT_copied, 2 * (u + 1))
                n = 0
                for g in range(2):
                    for i in range(2):
                        if n == 0 and steady:
                            pe.wait_ge(v_copied, 2 * u)
                        if n == 3 and steady == 2:
                            pe.wait_ge(attn_added, 2 * u - 3)
                        nc.tensor.matmul(psum[0:C, QK_BANKS[n], :], qkv_w[:, i, :],
                                         hT[:, g * SHARES:(g + 1) * SHARES],
                                         start=True, stop=True).then_inc(qk_done, 1)
                        n += 1

            def project_v(u):
                for quad in range(QUADS):
                    for w in range(2):
                        n = 2 * quad + w
                        last = nc.tensor.matmul(psum[:, V_BANKS[n // 4], (n % 4) * C:(n % 4 + 1) * C],
                                                hT[:, n * P:(n + 1) * P], qkv_w[:, 2, :],
                                                start=True, stop=True)
                    if quad % 2:
                        last.then_inc(v_done, 1)

            def score(u):
                pe.wait_ge(qk_copied, 4 * (u + 1))
                for quad in range(QUADS):
                    for parity in range(2):
                        tile = 2 * quad + parity
                        for w in range(2):
                            at = (4 * quad + 2 * w + parity) * WT
                            for h in range(HEADS):
                                rows = slice(KD * h, KD * (h + 1))
                                last = nc.tensor.matmul(
                                    psum[WT * w:WT * (w + 1), S_BANKS[h], tile * WT:(tile + 1) * WT],
                                    qT[rows, at:at + WT], kT[rows, at:at + WT], start=True, stop=True)
                last.then_inc(scores_done, 1)

            def transpose_probs(u):
                for h in range(HEADS):
                    if h > 0:
                        pe.wait_ge(qk_copied, 4 * (u + 1) + h)
                    pe.wait_ge(probs_ready, HEADS * u + h + 1)
                    for quad in range(QUADS):
                        last = nc.tensor.transpose(psum[:, PT_BANKS[h], quad * P:(quad + 1) * P],
                                                   probs[:, quad, h, :, :].rearrange("p a k -> p (a k)"),
                                                   ident[:, :])
                    last.then_inc(pt_done, 1)

            def attend(u):
                pe.wait_ge(v_copied, 2 * (u + 1))
                wait_apart(pe, pt_copied, HEADS * (u + 1))
                for quad in range(QUADS):
                    for w in range(2):
                        at = (2 * quad + w) * WT
                        for parity in range(2):
                            keys = slice(WT * parity, WT * (parity + 1))
                            for h in range(HEADS):
                                last = nc.tensor.matmul(
                                    psum[KD * h:KD * (h + 1), PV_BANKS[parity], at:at + WT],
                                    v[keys, quad, w, KD * h:KD * (h + 1)],
                                    probsT[keys, h, quad, WT * w:WT * (w + 1)], start=True, stop=True)
                last.then_inc(pv_done, 1)

            def project_out(u):
                pe.wait_ge(oT_copied, 2 * (u + 1))
                for c in range(TILES):
                    if c == 4:
                        pe.wait_ge(v_copied, 2 * (u + 1) + 1)
                    last = nc.tensor.matmul(psum[:, O_BANKS[c // 4], (c % 4) * C:(c % 4 + 1) * C],
                                            oT[:, c * P:(c + 1) * P], wo_w[:, :], start=True, stop=True)
                    if c % 4 == 3:
                        last.then_inc(o_done, 1)

            def transpose2(u, steady):
                pe.wait_ge(ln2_ready, u + 1)
                if steady:
                    pe.wait_ge(gelu_done, 2 * FCHUNKS * u - FCHUNKS)
                transpose_rows(T2_BANKS, t2_done)

            def up(u, part, steady):
                pe.wait_ge(h2T_copied, 2 * u + 1 + part)
                if part and steady:
                    pe.wait_ge(gelu_done, 2 * FCHUNKS * u)
                for j in range(FCHUNKS):
                    if part == 0 and j == 2:
                        pe.wait_ge(h2T_copied, 2 * u + 2)
                    nc.tensor.matmul(psum[:, UP_BANKS[part][j], :], w1_w[:, j * P:(j + 1) * P],
                                     h2T[:, part * SHARES:(part + 1) * SHARES],
                                     start=True, stop=True).then_inc(up_done, 1)

            def down(u, part, steady):
                pe.wait_ge(gelu_done, 2 * FCHUNKS * u + FCHUNKS * (part + 1))
                if steady:
                    pe.wait_ge(mlp_added, 2 * u - 1 + part)
                for t in range(TILES // 2):
                    c = part * (TILES // 2) + t
                    for j in range(FCHUNKS):
                        last = nc.tensor.matmul(psum[:, DOWN_BANKS[part], t * C:(t + 1) * C],
                                                gelu[:, j, c * P:(c + 1) * P], w2_w[:, j, :],
                                                start=(j == 0), stop=(j == FCHUNKS - 1))
                last.then_inc(down_done, 1)

            def mlp_step(u, first, last):
                up(u, 1, not first)
                if not last:
                    transpose2(u + 1, True)
                down(u, 0, not first)
                if not last:
                    up(u + 1, 0, True)
                down(u, 1, not first)

            transpose1(0, False)
            project_qk(0, 0)
            score(0)
            project_v(0)
            transpose1(1, False)
            project_qk(1, 1)

            with pe.Fori(0, BATCHES) as b:
                batch = b * BATCH
                with pe.Fori(0, BATCH) as j:
                    u = batch + j
                    transpose_probs(u)
                    score(u + 1)
                    attend(u)
                    project_v(u + 1)
                    transpose1(u + 2, True)
                    project_out(u)
                    project_qk(u + 2, 2)
                    wait_apart(pe, attn_added, 2 * (u + 1))
                pe.wait_ge(exp_done, HEADS * (batch + BATCH + 1))
                pe.wait_ge(qk_copied, 4 * (batch + BATCH + 2))
                pe.wait_ge(attn_added, 2 * (batch + BATCH))
                transpose2(batch, False)
                up(batch, 0, False)
                mlp_step(batch, True, False)
                with pe.Fori(1, BATCH - 1) as j:
                    mlp_step(batch + j, False, False)
                mlp_step(batch + BATCH - 1, False, True)
                pe.wait_ge(gelu_done, 2 * FCHUNKS * (batch + BATCH))
                wait_apart(pe, mlp_added, 2 * (batch + BATCH))

        @block.scalar
        def _(act):
            def rstd(log, stepped, sq, dst):
                nc.scalar.activation(log[:, :], sq[:, :], ACT.Ln, bias=eps_col[:, :], scale=1.0 / C)\
                    .then_inc(stepped, 1)

            def rstd1_of(u):
                act.wait_ge(ln1_step, LN_STEPS * (u + 1))
                rstd(log_var[0], log1_step, sq_dev[0], rstd1)
                act.wait_ge(log1_step, u + 1)
                nc.scalar.activation(rstd1[:, :], log_var[0][:, :], ACT.Exp, scale=-0.5).then_inc(rstd1_ready, 1)

            def rstd2_of(u):
                act.wait_ge(ln2_step, LN_STEPS * (u + 1))
                rstd(log_var[1], log2_step, sq_dev[1], rstd2)
                act.wait_ge(log2_step, u + 1)
                nc.scalar.activation(rstd2[:, u & (BATCH - 1), :], log_var[1][:, :], ACT.Exp, scale=-0.5)\
                    .then_inc(rstd2_ready, 1)

            def copy_qk(u):
                n = 0
                for g in range(2):
                    for dst in (qT, kT):
                        act.wait_ge(qk_done, 4 * u + n + 1)
                        nc.scalar.activation(dst[:, g * SHARES:(g + 1) * SHARES], psum[0:C, QK_BANKS[n], :],
                                             ACT.Copy).then_inc(qk_copied, 1)
                        n += 1

            def copy_probsT(u):
                for h in range(HEADS):
                    act.wait_ge(pt_done, HEADS * u + h + 1)
                    nc.scalar.activation(probsT[:, h, :, :].rearrange("p q k -> p (q k)"),
                                         psum[:, PT_BANKS[h], :], ACT.Copy).then_inc(pt_copied, 1)

            def exps(u):
                for h in range(HEADS):
                    act.wait_ge(bias_ready, HEADS * u + h + 1)
                    for tile in range(2 * QUADS):
                        last = nc.scalar.activation(
                            probs[:, tile // 2, h, tile % 2, :],
                            psum[:, S_BANKS[h], tile * WT:(tile + 1) * WT], ACT.Exp,
                            bias=exp_bias[:, h, tile:tile + 1], scale=SCALE,
                            accum_out=prob_sum[:, h, tile:tile + 1])
                    last.then_inc(exp_done, 1)

            def gelus(u, part):
                for j in range(FCHUNKS):
                    act.wait_ge(up_done, 2 * FCHUNKS * u + FCHUNKS * part + j + 1)
                    nc.scalar.activation(gelu[:, j, part * SHARES:(part + 1) * SHARES],
                                         psum[:, UP_BANKS[part][j], :], ACT.Gelu).then_inc(gelu_done, 1)

            act.wait_ge(rows_cleared, 6)
            act.dma_start(wo_w[ONES:ONES + 1, :], bo.rearrange("(a n) -> a n", a=1)).then_inc(weights_in, 16)
            act.wait_ge(consts_set, 5)
            rstd1_of(0)
            copy_qk(0)
            rstd1_of(1)
            exps(0)
            copy_qk(1)
            with act.Fori(0, BATCHES) as b:
                batch = b * BATCH
                with act.Fori(0, BATCH) as j:
                    u = batch + j
                    copy_probsT(u)
                    rstd1_of(u + 2)
                    exps(u + 1)
                    copy_qk(u + 2)
                    rstd2_of(u)
                with act.Fori(0, BATCH) as j:
                    gelus(batch + j, 0)
                    gelus(batch + j, 1)

        @block.vector
        def _(dve):
            nc.vector.memset(eps_col[:, :], EPS).then_inc(consts_set, 1)
            for rows in (qkv_w[C:P, :, :], wo_w[C:P, :], w1_w[C:P, :], hT[C:P, :], oT[C:P, :], h2T[C:P, :]):
                nc.vector.memset(rows, 0.0).then_inc(rows_cleared, 1)
            dve.wait_ge(rows_cleared, 6)
            for t in (hT, oT, h2T):
                nc.vector.memset(t[ONES:ONES + 1, :], 1.0).then_inc(consts_set, 1)
            dve.wait_ge(weights_in, 16 * (N_WEIGHT_DMAS + 1))
            nc.vector.tensor_scalar(qkv_w[0:C, :, :].rearrange("c i n -> c (i n)"),
                                    qkv_raw[:, :, :].rearrange("c i n -> c (i n)"),
                                    ln_cols[:, 0:1], None, ALU.mult).then_inc(weights_ready, 1)
            nc.vector.tensor_scalar(w1_w[0:C, :], w1_raw[:, :], ln_cols[:, 2:3], None, ALU.mult)\
                .then_inc(weights_ready, 1)
            dve.wait_ge(bias_folded, 1)
            dve.wait_ge(consts_set, 5)
            nc.vector.tensor_tensor(qkv_w[ONES:ONES + 1, :, :].rearrange("c i n -> c (i n)"),
                                    psum[ONES:ONES + 1, 0, 0:3 * C], bias_rows[ONES:ONES + 1, 0:3 * C],
                                    ALU.add).then_inc(weights_ready, 1)
            nc.vector.tensor_tensor(w1_w[ONES:ONES + 1, :], psum[ONES:ONES + 1, 1, 0:F],
                                    bias_rows[ONES:ONES + 1, 3 * C:3 * C + F], ALU.add)\
                .then_inc(weights_ready, 1)

            def slot_of(u):
                return u % SLOTS if isinstance(u, int) else u & (SLOTS - 1)

            def statistics(u, i, step, mean):
                at = LN_STEPS * u
                slot = slot_of(u)
                for c in range(TILES):
                    last = nc.vector.bn_stats(stats[i][:, c, :], stream[:, slot, c * C:(c + 1) * C])
                last.then_inc(step, 1)
                dve.wait_ge(step, at + 1)
                even, odd = stats[i][:, :, 1], stats[i][:, :, 4]
                nc.vector.tensor_tensor(mean_gap[i][:, :], even, odd, ALU.subtract).then_inc(step, 1)
                nc.vector.tensor_tensor(within[i][:, :], stats[i][:, :, 2], stats[i][:, :, 5], ALU.add)
                nc.vector.tensor_tensor(mean_sum[i][:, :], even, odd, ALU.add).then_inc(step, 1)
                dve.wait_ge(step, at + 2)
                nc.vector.scalar_tensor_tensor(between[i][:, :], mean_gap[i][:, :], C / 4, mean_gap[i][:, :],
                                               ALU.mult, ALU.mult).then_inc(step, 1)
                dve.wait_ge(step, at + 3)
                nc.vector.tensor_scalar(mean, mean_sum[i][:, :], 0.5, None, ALU.mult).then_inc(step, 1)
                dve.wait_ge(step, at + 4)
                nc.vector.tensor_tensor(sq_dev[i][:, :], within[i][:, :], between[i][:, :], ALU.add)\
                    .then_inc(step, 1)

            def normalise(u, mean, inv, ready):
                slot = slot_of(u)
                for c in range(TILES):
                    last = nc.vector.tensor_scalar(normed[:, c, :], stream[:, slot, c * C:(c + 1) * C],
                                                   mean[:, c:c + 1], inv[:, c:c + 1],
                                                   ALU.subtract, ALU.mult)
                last.then_inc(ready, 1)

            def statistics1(u, row, half):
                wait_apart(dve, x_loaded[half], 16 * LOAD_DMAS[half] * (row + 1))
                statistics(u, 0, ln1_step, mean1[:, :])

            def normalise1(u):
                dve.wait_ge(rstd1_ready, u + 1)
                normalise(u, mean1, rstd1, ln1_ready)

            def copy_hT(u):
                ordered = hT[0:C, :].rearrange("c (w k r) -> c k w r", w=WINDOWS, r=4)
                for g in range(2):
                    dve.wait_ge(t1_done, 2 * u + g + 1)
                    nc.vector.tensor_copy(
                        ordered[:, 8 * g:8 * (g + 1), :, :],
                        psum[0:C, T_BANKS[g], :].rearrange("c (k w r) -> c k w r", k=8, r=4))\
                        .then_inc(hT_copied, 1)

            def copy_v(u):
                for g in range(2):
                    dve.wait_ge(v_done, 2 * u + g + 1)
                    nc.vector.tensor_copy(v[:, 2 * g:2 * g + 2, :, :].rearrange("p q w c -> p (q w c)"),
                                          psum[:, V_BANKS[g], 0:GROUP]).then_inc(v_copied, 1)

            def maxima(u):
                dve.wait_ge(scores_done, u + 1)
                for h in range(HEADS):
                    nc.vector.tensor_reduce(neg_max[:, h, :],
                                            psum[:, S_BANKS[h], :].rearrange("p (t k) -> p t k", k=WT),
                                            AXIS.X, ALU.max, negate=True).then_inc(max_step, 1)
                    dve.wait_ge(max_step, HEADS * u + h + 1)
                    nc.vector.tensor_scalar(exp_bias[:, h, :], neg_max[:, h, :], SCALE, None, ALU.mult)\
                        .then_inc(bias_ready, 1)

            def invert_sums(u, steady):
                dve.wait_ge(exp_done, HEADS * (u + 1))
                if steady:
                    dve.wait_ge(probs_ready, HEADS * u)
                nc.vector.reciprocal(prob_inv[:, :, :].rearrange("p h t -> p (h t)"),
                                     prob_sum[:, :, :].rearrange("p h t -> p (h t)")).then_inc(inv_ready, 1)

            def copy_oT(u):
                dve.wait_ge(pv_done, u + 1)
                ordered = oT[0:C, :].rearrange("c (k n a r) -> c a n k r", k=16, a=2, r=4)
                for parity in range(2):
                    nc.vector.tensor_copy(
                        ordered[:, parity, :, :, :],
                        psum[0:C, PV_BANKS[parity], :].rearrange("c (n k r) -> c n k r", k=16, r=4))\
                        .then_inc(oT_copied, 1)

            def add_into_stream(u, banks, g, added):
                part = stream[:, slot_of(u), g * GROUP:(g + 1) * GROUP]
                nc.vector.tensor_tensor(part, part, psum[:, banks[g], 0:GROUP], ALU.add).then_inc(added, 1)

            def add_attention(u):
                for g in range(2):
                    dve.wait_ge(o_done, 2 * u + g + 1)
                    add_into_stream(u, O_BANKS, g, attn_added)
                wait_apart(dve, attn_added, 2 * (u + 1))
                statistics(u, 1, ln2_step, mean2[:, u & (BATCH - 1), :])

            def normalise2(u):
                dve.wait_ge(rstd2_ready, u + 1)
                nc.vector.tensor_copy(mean2_now[:, :], mean2[:, u & (BATCH - 1), :]).then_inc(copy_step, 1)
                nc.vector.tensor_copy(rstd2_now[:, :], rstd2[:, u & (BATCH - 1), :]).then_inc(copy_step, 1)
                dve.wait_ge(copy_step, 2 * (u + 1))
                normalise(u, mean2_now, rstd2_now, ln2_ready)

            def copy_h2T(u):
                for g in range(2):
                    dve.wait_ge(t2_done, 2 * u + g + 1)
                    nc.vector.tensor_copy(h2T[0:C, g * SHARES:(g + 1) * SHARES], psum[0:C, T2_BANKS[g], :])\
                        .then_inc(h2T_copied, 1)

            def add_mlp(u):
                dve.wait_ge(b2_added, u + 1)
                for g in range(2):
                    dve.wait_ge(down_done, 2 * u + g + 1)
                    add_into_stream(u, DOWN_BANKS, g, mlp_added)

            statistics1(0, 0, 0)
            normalise1(0)
            copy_hT(0)
            statistics1(1, 0, 1)
            maxima(0)
            normalise1(1)
            copy_v(0)
            copy_hT(1)
            invert_sums(0, False)
            with dve.Fori(0, BATCHES) as b:
                batch_row = b * BATCH_ROWS
                with dve.Fori(0, BATCH_ROWS) as r:
                    for half in (0, 1):
                        row = batch_row + r
                        u = 2 * row + half
                        statistics1(u + 2, row + 1, half)
                        maxima(u + 1)
                        normalise1(u + 2)
                        copy_oT(u)
                        copy_v(u + 1)
                        copy_hT(u + 2)
                        invert_sums(u + 1, True)
                        add_attention(u)
                batch = 2 * batch_row
                normalise2(batch)
                copy_h2T(batch)
                with dve.Fori(0, BATCH - 1) as j:
                    normalise2(batch + j + 1)
                    copy_h2T(batch + j + 1)
                    add_mlp(batch + j)
                add_mlp(batch + BATCH - 1)


_INS = ["x", "L0_conv_ln1_g", "L0_conv_ln1_b", "L0_conv_wq", "L0_conv_bq", "L0_conv_wk", "L0_conv_bk",
        "L0_conv_wv", "L0_conv_bv", "L0_conv_wo", "L0_conv_bo", "L0_conv_ln2_g", "L0_conv_ln2_b",
        "L0_conv_w1", "L0_conv_b1", "L0_conv_w2", "L0_conv_b2"]


def kernel(**inputs):
    import numpy as np
    import concourse.bacc as bacc
    from concourse.bass_utils import run_bass_kernel_spmd

    nc = bacc.Bacc("TRN2", target_bir_lowering=False, num_devices=1)
    arrays, args = {}, []
    for name in _INS:
        a = np.ascontiguousarray(inputs[name])
        arrays[f"in_{name}"] = a
        args.append(nc.dram_tensor(f"in_{name}", a.shape, mybir.dt.from_np(a.dtype), kind="ExternalInput").ap())
    out = nc.dram_tensor("out", (IMAGES, HEIGHT, WIDTH, C), FP32, kind="ExternalOutput").ap()
    swin_block(nc, *args, out)
    result = run_bass_kernel_spmd(nc, [arrays], core_ids=[0])
    return result.results[0]["out"]
```

```python
from contextlib import ExitStack

import concourse.bass as bass
from concourse import mybir

FP32 = mybir.dt.float32
FP32R = mybir.dt.float32r
ALU = mybir.AluOpType
ACT = mybir.ActivationFunctionType
AXIS = mybir.AxisListType

IMAGES, HEIGHT, WIDTH, C = 4, 256, 256, 96
HEADS, KD, WIN, SHIFT = 3, 32, 8, 4
F = 4 * C
FCHUNKS = F // 128
EPS = 1e-6
SCALE = KD ** -0.5
P = 128

WROWS = IMAGES * HEIGHT // WIN
UNITS = 2 * WROWS
WINDOWS = WIDTH // WIN // 2
WT = WIN * WIN
TOK = WINDOWS * WT
TILES = TOK // P
QUADS = WINDOWS // 4
BATCH = 16
BATCH_ROWS = BATCH // 2
BATCHES = UNITS // BATCH
SLOTS = 2 * BATCH
ROW = WIDTH * C
SEG = WIN * C
ONES = C
LOAD_DMAS = (2, 6)
SHARES = TOK // 2
GROUP = 4 * C
PART = QUADS


def swin_block(nc, x, ln1_g, ln1_b, wq, bq, wk, bk, wv, bv, wo, bo, ln2_g, ln2_b, w1, b1, w2, b2, out):
    x_rows = x.rearrange("b (g r) w c -> (b g) r (w c)", r=SHIFT)
    out_rows = out.rearrange("b (g r) w c -> (b g) r (w c)", r=SHIFT)

    with ExitStack() as ctx:
        def sb(name, *shape, dtype=FP32):
            return ctx.enter_context(nc.sbuf_tensor(name, list(shape), dtype))

        def sb_split(name, *shape):
            return [sb(f"{name}_{half}", *shape, dtype=FP32R) for half in ("upper", "lower")]

        def sem(name):
            return ctx.enter_context(nc.semaphore(name))

        stream = sb("stream", P, SLOTS, SEG)
        normed1 = sb("normed1", P, TILES, C)
        normed2 = sb("normed2", P, TILES, C)
        hT = sb("hT", P, TOK)
        qT = sb("qT", C, TOK)
        kT = sb("kT", C, TOK)
        v = sb("v", P, 2, QUADS, 2, C)
        probs = sb("probs", P, 2, HEADS, 2 * PART, WT)
        probsT = sb("probsT", P, HEADS, QUADS, P)
        oT = sb("oT", P, TOK)
        h2T = sb_split("h2T", P, TOK)
        gelu = sb("gelu", P, FCHUNKS, TOK)
        qkv_raw = sb("qkv_raw", C, 3, C)
        qkv_w = sb("qkv_w", P, 3, C)
        wo_w = sb("wo_w", P, C)
        w1_raw = sb("w1_raw", C, F)
        w1_w = sb("w1_w", P, F)
        w1_split = sb_split("w1_split", P, F)
        w2_w = sb("w2_w", P, FCHUNKS, C)
        b2_all = sb("b2_all", P, C)
        ln_cols = sb("ln_cols", C, 4)
        bias_rows = sb("bias_rows", P, 3 * C + F)
        ident = sb("ident", P, P)
        eps_col = sb("eps_col", P, 1)
        stats = [sb(f"stats{i}", P, TILES, 6) for i in (1, 2)]
        mean_sum = [sb(f"mean_sum{i}", P, TILES) for i in (1, 2)]
        mean_gap = [sb(f"mean_gap{i}", P, TILES) for i in (1, 2)]
        within = [sb(f"within{i}", P, TILES) for i in (1, 2)]
        between = [sb(f"between{i}", P, TILES) for i in (1, 2)]
        sq_dev = [sb(f"sq_dev{i}", P, TILES) for i in (1, 2)]
        log_var = [sb(f"log_var{i}", P, TILES) for i in (1, 2)]
        mean1 = sb("mean1", P, TILES)
        rstd1 = sb("rstd1", P, TILES)
        mean2 = sb("mean2", P, BATCH, TILES)
        rstd2 = sb("rstd2", P, BATCH, TILES)
        mean2_now = sb("mean2_now", P, TILES)
        rstd2_now = sb("rstd2_now", P, TILES)
        neg_max = sb("neg_max", P, HEADS, 2 * PART)
        exp_bias = sb("exp_bias", P, HEADS, 2 * PART)
        prob_sum = sb("prob_sum", P, HEADS, 2 * PART)
        prob_inv = sb("prob_inv", P, HEADS, 2 * PART)

        psum = ctx.enter_context(nc.psum_tensor("psum", [P, 8, 512], FP32))
        S_BANKS = ((0, 1, 2), (5, 6, 7))
        PT_BANKS = (3, 4, 0)
        T_BANKS = (3, 4)
        QK_BANKS = (3, 4, 2, 5)
        PV_BANKS = (0, 1)
        V_BANKS = (3, 4)
        O_BANKS = (6, 7)
        T2_BANKS = (0, 1)
        UP_BANKS = ((0, 2, 1), (3, 4, 5))
        DOWN_BANKS = (6, 7)

        weights_in = sem("weights_in")
        consts_set = sem("consts_set")
        passed = sem("passed")
        ident_zeroed = sem("ident_zeroed")
        rows_cleared = sem("rows_cleared")
        bias_folded = sem("bias_folded")
        weights_ready = sem("weights_ready")
        x_loaded = [sem("x_loaded_left"), sem("x_loaded_right")]
        stored = sem("stored")
        ln1_step = sem("ln1_step")
        ln2_step = sem("ln2_step")
        max_step = sem("max_step")
        copy_step = sem("copy_step")
        upper_step = sem("upper_step")
        split_step = sem("split_step")
        log1_step = sem("log1_step")
        log2_step = sem("log2_step")
        rstd1_ready = sem("rstd1_ready")
        ln1_ready = sem("ln1_ready")
        t1_done = sem("t1_done")
        hT_copied = sem("hT_copied")
        qk_done = sem("qk_done")
        qk_copied = sem("qk_copied")
        v_done = sem("v_done")
        v_copied = sem("v_copied")
        scores_done = sem("scores_done")
        bias_ready = sem("bias_ready")
        exp_done = sem("exp_done")
        inv_ready = sem("inv_ready")
        probs_ready = sem("probs_ready")
        pt_done = sem("pt_done")
        pt_copied = sem("pt_copied")
        pv_done = sem("pv_done")
        oT_copied = sem("oT_copied")
        o_done = sem("o_done")
        attn_added = sem("attn_added")
        sq2_ready = sem("sq2_ready")
        rstd2_ready = sem("rstd2_ready")
        ln2_ready = sem("ln2_ready")
        b2_added = sem("b2_added")
        t2_done = sem("t2_done")
        h2T_copied = sem("h2T_copied")
        up_done = sem("up_done")
        gelu_done = sem("gelu_done")
        down_done = sem("down_done")
        mlp_added = sem("mlp_added")

        N_WEIGHT_DMAS = 15
        LN_STEPS = 6

        block = ctx.enter_context(nc.Block())

        def wait_apart(eng, semaphore, count):
            eng.wait_ge(semaphore, count)
            eng.sem_inc(passed, 1)

        def pieces(row, half):
            upper = 2 * row + 1
            if isinstance(row, int):
                lower = 2 * ((row // 32) * 32 + (row + 1) % 32)
            else:
                lower = 2 * ((row & (WROWS - 32)) + ((row + 1) & 31))
            for part, group in ((0, upper), (1, lower)):
                first = 64 * part
                if half == 0:
                    yield group, SHIFT * C, first, WINDOWS, SEG, 0
                else:
                    yield group, SHIFT * C + WINDOWS * SEG, first, WINDOWS - 1, SEG, 0
                    edge = first + 4 * (WINDOWS - 1)
                    yield group, ROW - SHIFT * C, edge, 1, SHIFT * C, 0
                    yield group, 0, edge, 1, SHIFT * C, SHIFT * C

        def dram_and_sbuf(rows, row, half, slot):
            for group, col, first, n, width, at in pieces(row, half):
                dram = rows[group, :, col:col + n * width].rearrange("r (w e) -> w r e", e=width)
                yield dram, stream[first:first + 4 * n, slot, at:at + width]

        @block.sync
        def _(sp):
            for i, w in enumerate((wq, wk, wv)):
                sp.dma_start(qkv_raw[:, i, :], w.rearrange("c h d -> c (h d)")).then_inc(weights_in, 16)
            for i, b in enumerate((bq, bk, bv)):
                sp.dma_start(bias_rows[ONES:ONES + 1, i * C:(i + 1) * C],
                             b.rearrange("(a h) d -> a (h d)", a=1)).then_inc(weights_in, 16)
            sp.dma_start(bias_rows[ONES:ONES + 1, 3 * C:3 * C + F],
                         b1.rearrange("(a n) -> a n", a=1)).then_inc(weights_in, 16)
            sp.dma_start(w1_raw[:, :], w1).then_inc(weights_in, 16)
            for i, col in enumerate((ln1_g, ln1_b, ln2_g, ln2_b)):
                sp.dma_start(ln_cols[:, i:i + 1], col.rearrange("(c a) -> c a", a=1)).then_inc(weights_in, 16)
            sp.dma_start(w2_w[:, :, :], w2.rearrange("(j p) c -> p j c", p=P)).then_inc(weights_in, 16)
            sp.dma_start(b2_all[:, :], b2.partition_broadcast(P)).then_inc(weights_in, 16)
            sp.dma_start(wo_w[0:C, :], wo.rearrange("h d c -> (h d) c")).then_inc(weights_in, 16)

            def load(row, source_row, half):
                if not (isinstance(row, int) and row == 0):
                    wait_apart(sp, x_loaded[half], 16 * LOAD_DMAS[half] * row)
                slot = (2 * row + half) % SLOTS if isinstance(row, int) else (2 * row + half) & (SLOTS - 1)
                for dram, sbuf in dram_and_sbuf(x_rows, source_row, half, slot):
                    sp.dma_start(sbuf, dram).then_inc(x_loaded[half], 16)

            def store(row, half):
                wait_apart(sp, mlp_added, 2 * (2 * row + half + 1) + 1)
                slot = (2 * row + half) & (SLOTS - 1)
                for dram, sbuf in dram_and_sbuf(out_rows, row, half, slot):
                    sp.dma_start(dram, sbuf).then_inc(stored, 16)

            def store_batch(batch_row):
                with sp.Fori(0, BATCH_ROWS) as r:
                    for half in (0, 1):
                        store(batch_row + r, half)
                wait_apart(sp, stored, 16 * sum(LOAD_DMAS) * (batch_row + BATCH_ROWS))

            for half in (0, 1):
                load(0, 0, half)
            with sp.Fori(1, 2 * BATCH_ROWS) as row:
                for half in (0, 1):
                    load(row, row, half)
            with sp.Fori(0, BATCHES - 2) as b:
                store_batch(b * BATCH_ROWS)
                with sp.Fori(0, BATCH_ROWS) as r:
                    for half in (0, 1):
                        row = b * BATCH_ROWS + r + 2 * BATCH_ROWS
                        load(row, row, half)
            store_batch((BATCHES - 2) * BATCH_ROWS)
            for row, half in ((0, 0), (0, 1), (1, 0)):
                load(BATCHES * BATCH_ROWS + row, row, half)
            store_batch((BATCHES - 1) * BATCH_ROWS)

        @block.gpsimd
        def _(pool):
            nc.gpsimd.memset(ident[:, :], 0.0).then_inc(ident_zeroed, 1)
            pool.wait_ge(ident_zeroed, 1)
            nc.gpsimd.affine_select(out=ident[:, :], in_=ident[:, :], compare_op=ALU.not_equal, fill=1.0,
                                    base=0, pattern=[[-1, P]], channel_multiplier=1).then_inc(consts_set, 1)

            def normalise_probs(u, buffer):
                pool.wait_ge(inv_ready, u + 1)
                for h in range(HEADS):
                    block_h = probs[:, buffer, h, :, :]
                    inv = prob_inv[:, h, :].unsqueeze(2).to_broadcast((P, 2 * PART, WT))
                    nc.gpsimd.tensor_tensor(block_h, block_h, inv, ALU.mult).then_inc(probs_ready, 1)

            def add_b2(u):
                pool.wait_ge(ln2_ready, u + 1)
                now = stream[:, u & (SLOTS - 1), :].rearrange("p (t c) -> p t c", c=C)
                nc.gpsimd.tensor_tensor(now, now, b2_all[:, :].unsqueeze(1).to_broadcast((P, TILES, C)),
                                        ALU.add).then_inc(b2_added, 1)

            pool.wait_ge(weights_in, 16 * (N_WEIGHT_DMAS + 1))
            normalise_probs(0, 0)
            with pool.Fori(0, BATCHES) as b:
                batch = b * BATCH
                with pool.Fori(0, BATCH_ROWS) as r:
                    for half in (0, 1):
                        normalise_probs(batch + 2 * r + half + 1, 1 - half)
                with pool.Fori(0, BATCH) as j:
                    add_b2(batch + j)

        @block.tensor
        def _(pe):
            pe.wait_ge(weights_in, 16 * (N_WEIGHT_DMAS + 1))
            nc.tensor.matmul(psum[ONES:ONES + 1, 0, 0:3 * C], ln_cols[:, 1:2],
                             qkv_raw[:, :, :].rearrange("c i n -> c (i n)"), start=True, stop=True)
            nc.tensor.matmul(psum[ONES:ONES + 1, 1, 0:F], ln_cols[:, 3:4], w1_raw[:, :],
                             start=True, stop=True).then_inc(bias_folded, 1)
            pe.wait_ge(weights_ready, 5)
            pe.wait_ge(consts_set, 4)

            def transpose_rows(normed, banks, g, done):
                for t in range(TILES // 2):
                    last = nc.tensor.transpose(psum[0:C, banks[g], t * P:(t + 1) * P],
                                               normed[:, g * (TILES // 2) + t, :], ident[:, :])
                last.then_inc(done, 1)

            def transpose1(u, g, steady):
                if g == 0:
                    pe.wait_ge(ln1_ready, u + 1)
                if steady:
                    pe.wait_ge(pt_copied, HEADS * (u - 2) + g + 1)
                transpose_rows(normed1, T_BANKS, g, t1_done)

            def project_qk(u, n, steady):
                if n == 0:
                    pe.wait_ge(hT_copied, 2 * (u + 1))
                if n >= 2 and steady:
                    pe.wait_ge(exp_done, 2 * HEADS * (u - 1) + n + 1)
                group, which = divmod(n, 2)
                nc.tensor.matmul(psum[0:C, QK_BANKS[n], :], qkv_w[:, which, :],
                                 hT[:, group * SHARES:(group + 1) * SHARES],
                                 start=True, stop=True).then_inc(qk_done, 1)

            def project_v(u):
                for n in range(TILES):
                    if n % 4 == 0:
                        pe.wait_ge(qk_copied, 4 * u + n // 4 + 1)
                    last = nc.tensor.matmul(psum[:, V_BANKS[n // 4], (n % 4) * C:(n % 4 + 1) * C],
                                            hT[:, n * P:(n + 1) * P], qkv_w[:, 2, :],
                                            start=True, stop=True)
                    if n % 4 == 3:
                        last.then_inc(v_done, 1)

            def score(quad):
                part = quad // 2
                for parity in range(2):
                    tile = 2 * (quad % 2) + parity
                    for w in range(2):
                        at = (4 * quad + 2 * w + parity) * WT
                        for h in range(HEADS):
                            rows = slice(KD * h, KD * (h + 1))
                            last = nc.tensor.matmul(
                                psum[WT * w:WT * (w + 1), S_BANKS[part][h], tile * WT:(tile + 1) * WT],
                                qT[rows, at:at + WT], kT[rows, at:at + WT], start=True, stop=True)
                if quad % 2:
                    last.then_inc(scores_done, 1)

            def transpose_probs(u, h, buffer):
                pe.wait_ge(probs_ready, HEADS * u + h + 1)
                if h < 2:
                    pe.wait_ge(v_copied, 2 * (u + 1) + h + 1)
                else:
                    pe.wait_ge(exp_done, 2 * HEADS * (u + 1) + 1)
                for quad in range(QUADS):
                    last = nc.tensor.transpose(
                        psum[:, PT_BANKS[h], quad * P:(quad + 1) * P],
                        probs[:, buffer, h, 2 * quad:2 * quad + 2, :].rearrange("p a k -> p (a k)"),
                        ident[:, :])
                last.then_inc(pt_done, 1)

            def score_and_transpose(u, buffer, first):
                pe.wait_ge(qk_copied, 4 * (u + 2))
                score(0)
                if not first:
                    project_out(u - 1, 1)
                score(1)
                transpose_probs(u, 0, buffer)
                transpose_probs(u, 1, buffer)
                if first:
                    wait_apart(pe, mlp_added, 2 * u + 1)
                else:
                    wait_apart(pe, attn_added, 2 * u)
                score(2)
                transpose1(u + 2, 0, True)
                transpose1(u + 2, 1, True)
                score(3)
                transpose_probs(u, 2, buffer)

            def attend(quad, buffer):
                for w in range(2):
                    at = (2 * quad + w) * WT
                    for parity in range(2):
                        keys = slice(WT * parity, WT * (parity + 1))
                        for h in range(HEADS):
                            last = nc.tensor.matmul(
                                psum[KD * h:KD * (h + 1), PV_BANKS[parity], at:at + WT],
                                v[keys, buffer, quad, w, KD * h:KD * (h + 1)],
                                probsT[keys, h, quad, WT * w:WT * (w + 1)], start=True, stop=True)
                if quad == QUADS - 1:
                    last.then_inc(pv_done, 1)

            def project_qk_and_attend(u, buffer):
                project_qk(u + 2, 0, True)
                project_qk(u + 2, 1, True)
                pe.wait_ge(pt_copied, HEADS * (u + 1))
                wait_apart(pe, exp_done, 2 * HEADS * (u + 1) + 2)
                attend(0, buffer)
                attend(1, buffer)
                project_qk(u + 2, 2, True)
                attend(2, buffer)
                attend(3, buffer)
                project_qk(u + 2, 3, True)

            def project_out(u, g):
                if g == 0:
                    pe.wait_ge(oT_copied, 2 * (u + 1))
                pe.wait_ge(exp_done, 2 * HEADS * (u + 1) + 5 + g)
                for t in range(TILES // 2):
                    c = g * (TILES // 2) + t
                    last = nc.tensor.matmul(psum[:, O_BANKS[g], t * C:(t + 1) * C],
                                            oT[:, c * P:(c + 1) * P], wo_w[:, :], start=True, stop=True)
                last.then_inc(o_done, 1)

            def attention_step(u, half, first):
                score_and_transpose(u, half, first)
                project_qk_and_attend(u, half)
                project_v(u + 2)
                project_out(u, 0)

            def transpose2(u, steady):
                pe.wait_ge(ln2_ready, u + 1)
                if steady:
                    pe.wait_ge(gelu_done, 2 * FCHUNKS * u - FCHUNKS)
                for g in range(2):
                    transpose_rows(normed2, T2_BANKS, g, t2_done)

            def up(u, part, steady):
                pe.wait_ge(h2T_copied, 2 * u + 1 + part)
                if part and steady:
                    pe.wait_ge(gelu_done, 2 * FCHUNKS * u)
                for j in range(FCHUNKS):
                    if part == 0 and j == 2:
                        pe.wait_ge(h2T_copied, 2 * u + 2)
                    for step, (w, h) in enumerate(((0, 0), (1, 0), (0, 1))):
                        last = nc.tensor.matmul(psum[:, UP_BANKS[part][j], :],
                                                w1_split[w][:, j * P:(j + 1) * P],
                                                h2T[h][:, part * SHARES:(part + 1) * SHARES],
                                                start=(step == 0), stop=(step == 2))
                    last.then_inc(up_done, 1)

            def down(u, part, steady):
                pe.wait_ge(gelu_done, 2 * FCHUNKS * u + FCHUNKS * (part + 1))
                if steady:
                    pe.wait_ge(mlp_added, 2 * u + part)
                for t in range(TILES // 2):
                    c = part * (TILES // 2) + t
                    for j in range(FCHUNKS):
                        last = nc.tensor.matmul(psum[:, DOWN_BANKS[part], t * C:(t + 1) * C],
                                                gelu[:, j, c * P:(c + 1) * P], w2_w[:, j, :],
                                                start=(j == 0), stop=(j == FCHUNKS - 1))
                last.then_inc(down_done, 1)

            def mlp_step(u, first, last):
                up(u, 1, not first)
                if not last:
                    transpose2(u + 1, True)
                down(u, 0, not first)
                if not last:
                    up(u + 1, 0, True)
                down(u, 1, not first)

            for g in range(2):
                transpose1(0, g, False)
            for n in range(4):
                project_qk(0, n, False)
            project_v(0)
            pe.wait_ge(qk_copied, 4)
            for quad in range(QUADS):
                score(quad)
            pe.wait_ge(v_copied, 2)
            for g in range(2):
                transpose1(1, g, False)
            for n in range(4):
                project_qk(1, n, True)
            project_v(1)
            wait_apart(pe, exp_done, 2 * HEADS)

            with pe.Fori(0, BATCHES) as b:
                batch = b * BATCH
                attention_step(batch, 0, True)
                attention_step(batch + 1, 1, False)
                with pe.Fori(1, BATCH_ROWS) as r:
                    for half in (0, 1):
                        attention_step(batch + 2 * r + half, half, False)
                project_out(batch + BATCH - 1, 1)
                transpose2(batch, False)
                pe.wait_ge(exp_done, 2 * HEADS * (batch + BATCH + 1))
                pe.wait_ge(qk_copied, 4 * (batch + BATCH + 2))
                pe.wait_ge(v_copied, 2 * (batch + BATCH + 2))
                up(batch, 0, False)
                pe.wait_ge(attn_added, 2 * (batch + BATCH))
                mlp_step(batch, True, False)
                with pe.Fori(1, BATCH - 1) as j:
                    mlp_step(batch + j, False, False)
                mlp_step(batch + BATCH - 1, False, True)
                pe.wait_ge(gelu_done, 2 * FCHUNKS * (batch + BATCH))

        @block.scalar
        def _(act):
            def rstd(log, stepped, sq, dst):
                nc.scalar.activation(log[:, :], sq[:, :], ACT.Ln, bias=eps_col[:, :], scale=1.0 / C)\
                    .then_inc(stepped, 1)

            def rstd1_of(u):
                act.wait_ge(ln1_step, LN_STEPS * (u + 1))
                rstd(log_var[0], log1_step, sq_dev[0], rstd1)
                act.wait_ge(log1_step, u + 1)
                nc.scalar.activation(rstd1[:, :], log_var[0][:, :], ACT.Exp, scale=-0.5).then_inc(rstd1_ready, 1)

            def rstd2_of(u):
                act.wait_ge(ln2_step, LN_STEPS * (u + 1))
                rstd(log_var[1], log2_step, sq_dev[1], rstd2)
                act.wait_ge(log2_step, u + 1)
                nc.scalar.activation(rstd2[:, u & (BATCH - 1), :], log_var[1][:, :], ACT.Exp, scale=-0.5)\
                    .then_inc(rstd2_ready, 1)

            def copy_qk(u, n):
                act.wait_ge(qk_done, 4 * u + n + 1)
                group, which = divmod(n, 2)
                nc.scalar.activation((qT, kT)[which][:, group * SHARES:(group + 1) * SHARES],
                                     psum[0:C, QK_BANKS[n], :], ACT.Copy).then_inc(qk_copied, 1)

            def copy_probsT(u, h):
                act.wait_ge(pt_done, HEADS * u + h + 1)
                nc.scalar.activation(probsT[:, h, :, :].rearrange("p q k -> p (q k)"),
                                     psum[:, PT_BANKS[h], :], ACT.Copy).then_inc(pt_copied, 1)

            def exps(u, buffer, part, h):
                act.wait_ge(bias_ready, 2 * u + part + 1)
                for t in range(PART):
                    tile = PART * part + t
                    last = nc.scalar.activation(
                        probs[:, buffer, h, tile, :],
                        psum[:, S_BANKS[part][h], t * WT:(t + 1) * WT], ACT.Exp,
                        bias=exp_bias[:, h, tile:tile + 1], scale=SCALE,
                        accum_out=prob_sum[:, h, tile:tile + 1])
                last.then_inc(exp_done, 1)

            def attention_step(u, half, first):
                other = 1 - half
                copy_probsT(u, 0)
                copy_probsT(u, 1)
                act.wait_ge(inv_ready, u + 1)
                exps(u + 1, other, 0, 0)
                exps(u + 1, other, 0, 1)
                copy_probsT(u, 2)
                exps(u + 1, other, 0, 2)
                copy_qk(u + 2, 0)
                copy_qk(u + 2, 1)
                exps(u + 1, other, 1, 0)
                if not first:
                    rstd2_of(u - 1)
                exps(u + 1, other, 1, 1)
                rstd1_of(u + 3)
                copy_qk(u + 2, 2)
                exps(u + 1, other, 1, 2)
                copy_qk(u + 2, 3)

            def gelus(u, part):
                for j in range(FCHUNKS):
                    act.wait_ge(up_done, 2 * FCHUNKS * u + FCHUNKS * part + j + 1)
                    nc.scalar.activation(gelu[:, j, part * SHARES:(part + 1) * SHARES],
                                         psum[:, UP_BANKS[part][j], :], ACT.Gelu).then_inc(gelu_done, 1)

            act.wait_ge(rows_cleared, 5)
            act.dma_start(wo_w[ONES:ONES + 1, :], bo.rearrange("(a n) -> a n", a=1)).then_inc(weights_in, 16)
            act.wait_ge(consts_set, 4)
            nc.scalar.preload_act_table_set("natural_log_exp_and_others")
            rstd1_of(0)
            for n in range(4):
                copy_qk(0, n)
            rstd1_of(1)
            for part in range(2):
                for h in range(HEADS):
                    exps(0, 0, part, h)
            for n in range(4):
                copy_qk(1, n)
            rstd1_of(2)
            with act.Fori(0, BATCHES) as b:
                batch = b * BATCH
                nc.scalar.preload_act_table_set("natural_log_exp_and_others")
                attention_step(batch, 0, True)
                attention_step(batch + 1, 1, False)
                with act.Fori(1, BATCH_ROWS) as r:
                    for half in (0, 1):
                        attention_step(batch + 2 * r + half, half, False)
                rstd2_of(batch + BATCH - 1)
                nc.scalar.preload_act_table_set("gelu_and_others")
                with act.Fori(0, BATCH) as j:
                    gelus(batch + j, 0)
                    gelus(batch + j, 1)

        @block.vector
        def _(dve):
            nc.vector.memset(eps_col[:, :], EPS).then_inc(consts_set, 1)
            for rows in (qkv_w[C:P, :, :], wo_w[C:P, :], w1_w[C:P, :], hT[C:P, :], oT[C:P, :]):
                nc.vector.memset(rows, 0.0).then_inc(rows_cleared, 1)
            dve.wait_ge(rows_cleared, 5)
            for t in (hT, oT):
                nc.vector.memset(t[ONES:ONES + 1, :], 1.0).then_inc(consts_set, 1)
            dve.wait_ge(weights_in, 16 * (N_WEIGHT_DMAS + 1))
            nc.vector.tensor_scalar(qkv_w[0:C, :, :].rearrange("c i n -> c (i n)"),
                                    qkv_raw[:, :, :].rearrange("c i n -> c (i n)"),
                                    ln_cols[:, 0:1], None, ALU.mult).then_inc(weights_ready, 1)
            nc.vector.tensor_scalar(w1_w[0:C, :], w1_raw[:, :], ln_cols[:, 2:3], None, ALU.mult)\
                .then_inc(weights_ready, 1)
            dve.wait_ge(bias_folded, 1)
            dve.wait_ge(consts_set, 4)
            nc.vector.tensor_copy(h2T[0][C:P, :], oT[C:P, :])
            nc.vector.tensor_tensor(h2T[1][C:P, :], oT[C:P, :], oT[C:P, :], ALU.subtract)
            nc.vector.tensor_tensor(qkv_w[ONES:ONES + 1, :, :].rearrange("c i n -> c (i n)"),
                                    psum[ONES:ONES + 1, 0, 0:3 * C], bias_rows[ONES:ONES + 1, 0:3 * C],
                                    ALU.add).then_inc(weights_ready, 1)
            nc.vector.tensor_tensor(w1_w[ONES:ONES + 1, :], psum[ONES:ONES + 1, 1, 0:F],
                                    bias_rows[ONES:ONES + 1, 3 * C:3 * C + F], ALU.add)\
                .then_inc(weights_ready, 1)
            dve.wait_ge(weights_ready, 4)
            nc.vector.tensor_copy(w1_split[0][:, :], w1_w[:, :]).then_inc(split_step, 1)
            dve.wait_ge(split_step, 1)
            nc.vector.tensor_tensor(w1_split[1][:, :], w1_w[:, :], w1_split[0][:, :], ALU.subtract)\
                .then_inc(weights_ready, 1)

            def slot_of(u):
                return u % SLOTS if isinstance(u, int) else u & (SLOTS - 1)

            def statistics(u, i, step, mean):
                at = LN_STEPS * u
                slot = slot_of(u)
                for c in range(TILES):
                    last = nc.vector.bn_stats(stats[i][:, c, :], stream[:, slot, c * C:(c + 1) * C])
                last.then_inc(step, 1)
                dve.wait_ge(step, at + 1)
                even, odd = stats[i][:, :, 1], stats[i][:, :, 4]
                nc.vector.tensor_tensor(mean_gap[i][:, :], even, odd, ALU.subtract).then_inc(step, 1)
                nc.vector.tensor_tensor(within[i][:, :], stats[i][:, :, 2], stats[i][:, :, 5], ALU.add)
                nc.vector.tensor_tensor(mean_sum[i][:, :], even, odd, ALU.add).then_inc(step, 1)
                dve.wait_ge(step, at + 2)
                nc.vector.scalar_tensor_tensor(between[i][:, :], mean_gap[i][:, :], C / 4, mean_gap[i][:, :],
                                               ALU.mult, ALU.mult).then_inc(step, 1)
                dve.wait_ge(step, at + 3)
                nc.vector.tensor_scalar(mean, mean_sum[i][:, :], 0.5, None, ALU.mult).then_inc(step, 1)
                dve.wait_ge(step, at + 4)
                nc.vector.tensor_tensor(sq_dev[i][:, :], within[i][:, :], between[i][:, :], ALU.add)\
                    .then_inc(step, 1)

            def normalise(u, normed, mean, inv, ready):
                slot = slot_of(u)
                for c in range(TILES):
                    last = nc.vector.tensor_scalar(normed[:, c, :], stream[:, slot, c * C:(c + 1) * C],
                                                   mean[:, c:c + 1], inv[:, c:c + 1],
                                                   ALU.subtract, ALU.mult)
                last.then_inc(ready, 1)

            def statistics1(u, row, half):
                wait_apart(dve, x_loaded[half], 16 * LOAD_DMAS[half] * (row + 1))
                statistics(u, 0, ln1_step, mean1[:, :])

            def normalise1(u):
                dve.wait_ge(rstd1_ready, u + 1)
                normalise(u, normed1, mean1, rstd1, ln1_ready)

            def copy_hT(u):
                ordered = hT[0:C, :].rearrange("c (w k r) -> c k w r", w=WINDOWS, r=4)
                for g in range(2):
                    dve.wait_ge(t1_done, 2 * u + g + 1)
                    nc.vector.tensor_copy(
                        ordered[:, 8 * g:8 * (g + 1), :, :],
                        psum[0:C, T_BANKS[g], :].rearrange("c (k w r) -> c k w r", k=8, r=4))\
                        .then_inc(hT_copied, 1)

            def copy_v(u, buffer, g):
                dve.wait_ge(v_done, 2 * u + g + 1)
                nc.vector.tensor_copy(v[:, buffer, 2 * g:2 * g + 2, :, :].rearrange("p q w c -> p (q w c)"),
                                      psum[:, V_BANKS[g], 0:GROUP]).then_inc(v_copied, 1)

            def maxima(u, part):
                dve.wait_ge(scores_done, 2 * u + part + 1)
                tiles = slice(PART * part, PART * (part + 1))
                first = S_BANKS[part][0]
                nc.vector.tensor_reduce(
                    neg_max[:, :, tiles],
                    psum[:, first:first + HEADS, 0:PART * WT].rearrange("p h (t k) -> p h t k", k=WT),
                    AXIS.X, ALU.max, negate=True).then_inc(max_step, 1)
                dve.wait_ge(max_step, 2 * u + part + 1)
                nc.vector.tensor_scalar(exp_bias[:, :, tiles], neg_max[:, :, tiles], SCALE, None, ALU.mult)\
                    .then_inc(bias_ready, 1)

            def invert_sums(u, steady):
                dve.wait_ge(exp_done, 2 * HEADS * (u + 1))
                if steady:
                    dve.wait_ge(probs_ready, HEADS * u)
                nc.vector.reciprocal(prob_inv[:, :, :].rearrange("p h t -> p (h t)"),
                                     prob_sum[:, :, :].rearrange("p h t -> p (h t)")).then_inc(inv_ready, 1)

            def copy_oT(u):
                dve.wait_ge(pv_done, u + 1)
                ordered = oT[0:C, :].rearrange("c (k n a r) -> c a n k r", k=16, a=2, r=4)
                for parity in range(2):
                    nc.vector.tensor_copy(
                        ordered[:, parity, :, :, :],
                        psum[0:C, PV_BANKS[parity], :].rearrange("c (n k r) -> c n k r", k=16, r=4))\
                        .then_inc(oT_copied, 1)

            def add_into_stream(u, banks, g, added):
                part = stream[:, slot_of(u), g * GROUP:(g + 1) * GROUP]
                nc.vector.tensor_tensor(part, part, psum[:, banks[g], 0:GROUP], ALU.add).then_inc(added, 1)

            def add_attention(u, g):
                dve.wait_ge(o_done, 2 * u + g + 1)
                add_into_stream(u, O_BANKS, g, attn_added)

            def statistics2(u):
                wait_apart(dve, attn_added, 2 * (u + 1))
                statistics(u, 1, ln2_step, mean2[:, u & (BATCH - 1), :])

            def normalise2(u):
                dve.wait_ge(rstd2_ready, u + 1)
                nc.vector.tensor_copy(mean2_now[:, :], mean2[:, u & (BATCH - 1), :]).then_inc(copy_step, 1)
                nc.vector.tensor_copy(rstd2_now[:, :], rstd2[:, u & (BATCH - 1), :]).then_inc(copy_step, 1)
                dve.wait_ge(copy_step, 2 * (u + 1))
                normalise(u, normed2, mean2_now, rstd2_now, ln2_ready)

            def copy_h2T(u):
                tokens = [slice(g * SHARES, (g + 1) * SHARES) for g in range(2)]
                for g in range(2):
                    dve.wait_ge(t2_done, 2 * u + g + 1)
                    nc.vector.tensor_copy(h2T[0][0:C, tokens[g]], psum[0:C, T2_BANKS[g], :])\
                        .then_inc(upper_step, 1)
                for g in range(2):
                    dve.wait_ge(upper_step, 2 * u + g + 1)
                    nc.vector.tensor_tensor(h2T[1][0:C, tokens[g]], psum[0:C, T2_BANKS[g], :],
                                            h2T[0][0:C, tokens[g]], ALU.subtract).then_inc(h2T_copied, 1)

            def add_mlp(u):
                dve.wait_ge(b2_added, u + 1)
                for g in range(2):
                    dve.wait_ge(down_done, 2 * u + g + 1)
                    add_into_stream(u, DOWN_BANKS, g, mlp_added)

            dve.sem_inc(mlp_added, 1)
            statistics1(0, 0, 0)
            normalise1(0)
            copy_hT(0)
            statistics1(1, 0, 1)
            normalise1(1)
            for g in range(2):
                copy_v(0, 0, g)
            for part in range(2):
                maxima(0, part)
            copy_hT(1)
            statistics1(2, 1, 0)
            normalise1(2)
            invert_sums(0, False)
            for g in range(2):
                copy_v(1, 1, g)

            def attention_step(row, half, first):
                u = 2 * row + half
                if not first:
                    add_attention(u - 1, 1)
                maxima(u + 1, 0)
                copy_hT(u + 2)
                maxima(u + 1, 1)
                if not first:
                    statistics2(u - 1)
                statistics1(u + 3, row + 1 + half, 1 - half)
                copy_oT(u)
                normalise1(u + 3)
                invert_sums(u + 1, True)
                for g in range(2):
                    copy_v(u + 2, half, g)
                add_attention(u, 0)

            with dve.Fori(0, BATCHES) as b:
                batch_row = b * BATCH_ROWS
                attention_step(batch_row, 0, True)
                attention_step(batch_row, 1, False)
                batch = 2 * batch_row
                normalise2(batch)
                with dve.Fori(1, BATCH_ROWS) as r:
                    for half in (0, 1):
                        attention_step(batch_row + r, half, False)
                add_attention(batch + BATCH - 1, 1)
                copy_h2T(batch)
                statistics2(batch + BATCH - 1)
                normalise2(batch + 1)
                with dve.Fori(0, BATCH - 2) as j:
                    copy_h2T(batch + j + 1)
                    normalise2(batch + j + 2)
                    add_mlp(batch + j)
                copy_h2T(batch + BATCH - 1)
                add_mlp(batch + BATCH - 2)
                add_mlp(batch + BATCH - 1)


_INS = ["x", "L0_conv_ln1_g", "L0_conv_ln1_b", "L0_conv_wq", "L0_conv_bq", "L0_conv_wk", "L0_conv_bk",
        "L0_conv_wv", "L0_conv_bv", "L0_conv_wo", "L0_conv_bo", "L0_conv_ln2_g", "L0_conv_ln2_b",
        "L0_conv_w1", "L0_conv_b1", "L0_conv_w2", "L0_conv_b2"]


def kernel(**inputs):
    import numpy as np
    import concourse.bacc as bacc
    from concourse.bass_utils import run_bass_kernel_spmd

    nc = bacc.Bacc("TRN2", target_bir_lowering=False, num_devices=1)
    arrays, args = {}, []
    for name in _INS:
        a = np.ascontiguousarray(inputs[name])
        arrays[f"in_{name}"] = a
        args.append(nc.dram_tensor(f"in_{name}", a.shape, mybir.dt.from_np(a.dtype), kind="ExternalInput").ap())
    out = nc.dram_tensor("out", (IMAGES, HEIGHT, WIDTH, C), FP32, kind="ExternalOutput").ap()
    swin_block(nc, *args, out)
    result = run_bass_kernel_spmd(nc, [arrays], core_ids=[0])
    return result.results[0]["out"]
```

```python
from contextlib import ExitStack

import concourse.bass as bass
from concourse import mybir

FP32 = mybir.dt.float32
FP32R = mybir.dt.float32r
ALU = mybir.AluOpType
ACT = mybir.ActivationFunctionType
AXIS = mybir.AxisListType

IMAGES, HEIGHT, WIDTH, C = 4, 256, 256, 96
HEADS, KD, WIN, SHIFT = 3, 32, 8, 4
F = 4 * C
FCHUNKS = F // 128
EPS = 1e-6
SCALE = KD ** -0.5
P = 128

WROWS = IMAGES * HEIGHT // WIN
UNITS = 2 * WROWS
WINDOWS = WIDTH // WIN // 2
WT = WIN * WIN
TOK = WINDOWS * WT
TILES = TOK // P
QUADS = WINDOWS // 4
BATCH = 16
BATCH_ROWS = BATCH // 2
BATCHES = UNITS // BATCH
SLOTS = 2 * BATCH
ROW = WIDTH * C
SEG = WIN * C
ONES = C
LOAD_DMAS = (2, 6)
SHARES = TOK // 2
GROUP = 4 * C
SPLIT_STEPS = ((0, 0), (1, 0), (0, 1))
PART = QUADS


def swin_block(nc, x, ln1_g, ln1_b, wq, bq, wk, bk, wv, bv, wo, bo, ln2_g, ln2_b, w1, b1, w2, b2, out):
    x_rows = x.rearrange("b (g r) w c -> (b g) r (w c)", r=SHIFT)
    out_rows = out.rearrange("b (g r) w c -> (b g) r (w c)", r=SHIFT)

    with ExitStack() as ctx:
        def sb(name, *shape, dtype=FP32):
            return ctx.enter_context(nc.sbuf_tensor(name, list(shape), dtype))

        def sb_split(name, *shape):
            return [sb(f"{name}_{half}", *shape, dtype=FP32R) for half in ("upper", "lower")]

        def sem(name):
            return ctx.enter_context(nc.semaphore(name))

        stream = sb("stream", P, SLOTS, SEG)
        normed1 = sb("normed1", P, TILES, C)
        normed2 = sb("normed2", P, TILES, C)
        hT = sb("hT", P, TOK)
        hT_split = sb_split("hT", P, TOK)
        qT = sb("qT", C, TOK)
        kT = sb("kT", C, TOK)
        v = sb("v", P, 2, QUADS, 2, C)
        probs = sb("probs", P, 2, HEADS, 2 * PART, WT)
        probsT = sb("probsT", P, HEADS, QUADS, P)
        oT = sb("oT", P, TOK)
        h2T = sb_split("h2T", P, TOK)
        gelu = sb("gelu", P, FCHUNKS, TOK)
        qkv_raw = sb("qkv_raw", C, 3, C)
        qkv_w = sb("qkv_w", P, 3, C)
        qk_split = sb_split("qk_split", P, 2, C)
        wo_w = sb("wo_w", P, C)
        w1_raw = sb("w1_raw", C, F)
        w1_w = sb("w1_w", P, F)
        w1_split = sb_split("w1_split", P, F)
        w2_w = sb("w2_w", P, FCHUNKS, C)
        b2_all = sb("b2_all", P, C)
        ln_cols = sb("ln_cols", C, 4)
        bias_rows = sb("bias_rows", P, 3 * C + F)
        ident = sb("ident", P, P)
        eps_col = sb("eps_col", P, 1)
        stats = [sb(f"stats{i}", P, TILES, 6) for i in (1, 2)]
        mean_sum = [sb(f"mean_sum{i}", P, TILES) for i in (1, 2)]
        mean_gap = [sb(f"mean_gap{i}", P, TILES) for i in (1, 2)]
        within = [sb(f"within{i}", P, TILES) for i in (1, 2)]
        between = [sb(f"between{i}", P, TILES) for i in (1, 2)]
        sq_dev = [sb(f"sq_dev{i}", P, TILES) for i in (1, 2)]
        log_var = [sb(f"log_var{i}", P, TILES) for i in (1, 2)]
        mean1 = sb("mean1", P, TILES)
        rstd1 = sb("rstd1", P, TILES)
        mean2 = sb("mean2", P, BATCH, TILES)
        rstd2 = sb("rstd2", P, BATCH, TILES)
        mean2_now = sb("mean2_now", P, TILES)
        rstd2_now = sb("rstd2_now", P, TILES)
        neg_max = sb("neg_max", P, HEADS, 2 * PART)
        exp_bias = sb("exp_bias", P, HEADS, 2 * PART)
        prob_sum = sb("prob_sum", P, HEADS, 2 * PART)
        prob_inv = sb("prob_inv", P, HEADS, 2 * PART)

        psum = ctx.enter_context(nc.psum_tensor("psum", [P, 8, 512], FP32))
        S_BANKS = ((0, 1, 2), (5, 6, 7))
        PT_BANKS = (3, 4, 0)
        T_BANKS = (3, 4)
        QK_BANKS = (3, 4, 2, 5)
        PV_BANKS = (0, 1)
        V_BANKS = (3, 4)
        O_BANKS = (6, 7)
        T2_BANKS = (0, 1)
        UP_BANKS = ((0, 2, 1), (3, 4, 5))
        DOWN_BANKS = (6, 7)

        weights_in = sem("weights_in")
        consts_set = sem("consts_set")
        passed = sem("passed")
        ident_zeroed = sem("ident_zeroed")
        rows_cleared = sem("rows_cleared")
        bias_folded = sem("bias_folded")
        weights_ready = sem("weights_ready")
        x_loaded = [sem("x_loaded_left"), sem("x_loaded_right")]
        stored = sem("stored")
        ln1_step = sem("ln1_step")
        ln2_step = sem("ln2_step")
        max_step = sem("max_step")
        copy_step = sem("copy_step")
        centre_step = sem("centre_step")
        upper_step = sem("upper_step")
        split_step = sem("split_step")
        log1_step = sem("log1_step")
        log2_step = sem("log2_step")
        rstd1_ready = sem("rstd1_ready")
        ln1_ready = sem("ln1_ready")
        t1_done = sem("t1_done")
        hT_upper_copied = sem("hT_upper_copied")
        hT_copied = sem("hT_copied")
        hT_united = sem("hT_united")
        qk_done = sem("qk_done")
        qk_copied = sem("qk_copied")
        v_done = sem("v_done")
        v_copied = sem("v_copied")
        scores_done = sem("scores_done")
        bias_ready = sem("bias_ready")
        exp_done = sem("exp_done")
        inv_ready = sem("inv_ready")
        probs_ready = sem("probs_ready")
        pt_done = sem("pt_done")
        pt_copied = sem("pt_copied")
        pv_done = sem("pv_done")
        oT_copied = sem("oT_copied")
        o_done = sem("o_done")
        attn_added = sem("attn_added")
        rstd2_ready = sem("rstd2_ready")
        ln2_ready = sem("ln2_ready")
        b2_added = sem("b2_added")
        t2_done = sem("t2_done")
        h2T_copied = sem("h2T_copied")
        up_done = sem("up_done")
        gelu_done = sem("gelu_done")
        down_done = sem("down_done")
        mlp_added = sem("mlp_added")

        N_WEIGHT_DMAS = 15
        LN_STEPS = 6

        block = ctx.enter_context(nc.Block())

        def wait_apart(eng, semaphore, count):
            eng.wait_ge(semaphore, count)
            eng.sem_inc(passed, 1)

        def pieces(row, half):
            upper = 2 * row + 1
            if isinstance(row, int):
                lower = 2 * ((row // 32) * 32 + (row + 1) % 32)
            else:
                lower = 2 * ((row & (WROWS - 32)) + ((row + 1) & 31))
            for part, group in ((0, upper), (1, lower)):
                first = 64 * part
                if half == 0:
                    yield group, SHIFT * C, first, WINDOWS, SEG, 0
                else:
                    yield group, SHIFT * C + WINDOWS * SEG, first, WINDOWS - 1, SEG, 0
                    edge = first + 4 * (WINDOWS - 1)
                    yield group, ROW - SHIFT * C, edge, 1, SHIFT * C, 0
                    yield group, 0, edge, 1, SHIFT * C, SHIFT * C

        def dram_and_sbuf(rows, row, half, slot):
            for group, col, first, n, width, at in pieces(row, half):
                dram = rows[group, :, col:col + n * width].rearrange("r (w e) -> w r e", e=width)
                yield dram, stream[first:first + 4 * n, slot, at:at + width]

        @block.sync
        def _(sp):
            for i, w in enumerate((wq, wk, wv)):
                sp.dma_start(qkv_raw[:, i, :], w.rearrange("c h d -> c (h d)")).then_inc(weights_in, 16)
            for i, b in enumerate((bq, bk, bv)):
                sp.dma_start(bias_rows[ONES:ONES + 1, i * C:(i + 1) * C],
                             b.rearrange("(a h) d -> a (h d)", a=1)).then_inc(weights_in, 16)
            sp.dma_start(bias_rows[ONES:ONES + 1, 3 * C:3 * C + F],
                         b1.rearrange("(a n) -> a n", a=1)).then_inc(weights_in, 16)
            sp.dma_start(w1_raw[:, :], w1).then_inc(weights_in, 16)
            for i, col in enumerate((ln1_g, ln1_b, ln2_g, ln2_b)):
                sp.dma_start(ln_cols[:, i:i + 1], col.rearrange("(c a) -> c a", a=1)).then_inc(weights_in, 16)
            sp.dma_start(w2_w[:, :, :], w2.rearrange("(j p) c -> p j c", p=P)).then_inc(weights_in, 16)
            sp.dma_start(b2_all[:, :], b2.partition_broadcast(P)).then_inc(weights_in, 16)
            sp.dma_start(wo_w[0:C, :], wo.rearrange("h d c -> (h d) c")).then_inc(weights_in, 16)

            def load(row, source_row, half):
                if not (isinstance(row, int) and row == 0):
                    wait_apart(sp, x_loaded[half], 16 * LOAD_DMAS[half] * row)
                slot = (2 * row + half) % SLOTS if isinstance(row, int) else (2 * row + half) & (SLOTS - 1)
                for dram, sbuf in dram_and_sbuf(x_rows, source_row, half, slot):
                    sp.dma_start(sbuf, dram).then_inc(x_loaded[half], 16)

            def store(row, half):
                wait_apart(sp, mlp_added, 2 * (2 * row + half + 1) + 1)
                slot = (2 * row + half) & (SLOTS - 1)
                for dram, sbuf in dram_and_sbuf(out_rows, row, half, slot):
                    sp.dma_start(dram, sbuf).then_inc(stored, 16)

            def store_batch(batch_row):
                with sp.Fori(0, BATCH_ROWS) as r:
                    for half in (0, 1):
                        store(batch_row + r, half)
                wait_apart(sp, stored, 16 * sum(LOAD_DMAS) * (batch_row + BATCH_ROWS))

            for half in (0, 1):
                load(0, 0, half)
            with sp.Fori(1, 2 * BATCH_ROWS) as row:
                for half in (0, 1):
                    load(row, row, half)
            with sp.Fori(0, BATCHES - 2) as b:
                store_batch(b * BATCH_ROWS)
                with sp.Fori(0, BATCH_ROWS) as r:
                    for half in (0, 1):
                        row = b * BATCH_ROWS + r + 2 * BATCH_ROWS
                        load(row, row, half)
            store_batch((BATCHES - 2) * BATCH_ROWS)
            for row, half in ((0, 0), (0, 1), (1, 0)):
                load(BATCHES * BATCH_ROWS + row, row, half)
            store_batch((BATCHES - 1) * BATCH_ROWS)

        @block.gpsimd
        def _(pool):
            nc.gpsimd.memset(ident[:, :], 0.0).then_inc(ident_zeroed, 1)
            pool.wait_ge(ident_zeroed, 1)
            nc.gpsimd.affine_select(out=ident[:, :], in_=ident[:, :], compare_op=ALU.not_equal, fill=1.0,
                                    base=0, pattern=[[-1, P]], channel_multiplier=1).then_inc(consts_set, 1)

            def normalise_probs(u, buffer):
                for h in range(HEADS):
                    if h != 1:
                        pool.wait_ge(inv_ready, 2 * u + (1 if h == 0 else 2))
                    block_h = probs[:, buffer, h, :, :]
                    inv = prob_inv[:, h, :].unsqueeze(2).to_broadcast((P, 2 * PART, WT))
                    nc.gpsimd.tensor_tensor(block_h, block_h, inv, ALU.mult).then_inc(probs_ready, 1)

            def unite_hT(u):
                pool.wait_ge(hT_copied, 2 * (u + 1))
                if not (isinstance(u, int) and u == 0):
                    pool.wait_ge(v_done, 2 * u)
                nc.gpsimd.tensor_tensor(hT[0:C, :], hT_split[0][0:C, :], hT_split[1][0:C, :], ALU.add)\
                    .then_inc(hT_united, 1)

            def normalise2(b):
                u = b * BATCH

                def per_tile(stat):
                    return stat[:, 0, :].unsqueeze(2).to_broadcast((P, TILES, C))

                pool.wait_ge(rstd2_ready, u + 1)
                nc.gpsimd.tensor_tensor(normed2[:, :, :],
                                        stream[:, u & (SLOTS - 1), :].rearrange("p (t c) -> p t c", c=C),
                                        per_tile(mean2), ALU.subtract).then_inc(centre_step, 1)
                pool.wait_ge(centre_step, b + 1)
                nc.gpsimd.tensor_tensor(normed2[:, :, :], normed2[:, :, :], per_tile(rstd2), ALU.mult)\
                    .then_inc(ln2_ready, 1)

            def add_b2(u):
                pool.wait_ge(ln2_ready, u + 1)
                now = stream[:, u & (SLOTS - 1), :].rearrange("p (t c) -> p t c", c=C)
                nc.gpsimd.tensor_tensor(now, now, b2_all[:, :].unsqueeze(1).to_broadcast((P, TILES, C)),
                                        ALU.add).then_inc(b2_added, 1)

            pool.wait_ge(weights_in, 16 * (N_WEIGHT_DMAS + 1))
            unite_hT(0)
            unite_hT(1)
            normalise_probs(0, 0)
            with pool.Fori(0, BATCHES) as b:
                batch = b * BATCH
                unite_hT(batch + 2)
                normalise_probs(batch + 1, 1)
                unite_hT(batch + 3)
                normalise2(b)
                normalise_probs(batch + 2, 0)
                with pool.Fori(1, BATCH_ROWS) as r:
                    for half in (0, 1):
                        u = batch + 2 * r + half
                        unite_hT(u + 2)
                        normalise_probs(u + 1, 1 - half)
                with pool.Fori(0, BATCH) as j:
                    add_b2(batch + j)

        @block.tensor
        def _(pe):
            pe.wait_ge(weights_in, 16 * (N_WEIGHT_DMAS + 1))
            nc.tensor.matmul(psum[ONES:ONES + 1, 0, 0:3 * C], ln_cols[:, 1:2],
                             qkv_raw[:, :, :].rearrange("c i n -> c (i n)"), start=True, stop=True)
            nc.tensor.matmul(psum[ONES:ONES + 1, 1, 0:F], ln_cols[:, 3:4], w1_raw[:, :],
                             start=True, stop=True).then_inc(bias_folded, 1)
            pe.wait_ge(weights_ready, 6)
            pe.wait_ge(consts_set, 4)

            def transpose_rows(normed, banks, g, done):
                for t in range(TILES // 2):
                    last = nc.tensor.transpose(psum[0:C, banks[g], t * P:(t + 1) * P],
                                               normed[:, g * (TILES // 2) + t, :], ident[:, :])
                last.then_inc(done, 1)

            def transpose1(u, g, steady):
                if g == 0:
                    pe.wait_ge(ln1_ready, u + 1)
                if steady:
                    pe.wait_ge(v_copied, 2 * (u - 1) + g + 1)
                transpose_rows(normed1, T_BANKS, g, t1_done)

            def project_qk(u, n, steady):
                if n == 0:
                    pe.wait_ge(hT_copied, 2 * (u + 1))
                if n < 2 and not (isinstance(u, int) and u < 2):
                    pe.wait_ge(pt_copied, HEADS * (u - 2) + n + 1)
                if n >= 2 and steady:
                    pe.wait_ge(exp_done, 2 * HEADS * (u - 1) + n + 1)
                group, which = divmod(n, 2)
                for step, (w, h) in enumerate(SPLIT_STEPS):
                    last = nc.tensor.matmul(psum[0:C, QK_BANKS[n], :], qk_split[w][:, which, :],
                                            hT_split[h][:, group * SHARES:(group + 1) * SHARES],
                                            start=(step == 0), stop=(step == 2))
                last.then_inc(qk_done, 1)

            def project_v(u):
                pe.wait_ge(hT_united, u + 1)
                for n in range(TILES):
                    if n % 4 == 0:
                        pe.wait_ge(qk_copied, 4 * u + n // 4 + 1)
                    last = nc.tensor.matmul(psum[:, V_BANKS[n // 4], (n % 4) * C:(n % 4 + 1) * C],
                                            hT[:, n * P:(n + 1) * P], qkv_w[:, 2, :],
                                            start=True, stop=True)
                    if n % 4 == 3:
                        last.then_inc(v_done, 1)

            def score(quad):
                part = quad // 2
                for parity in range(2):
                    tile = 2 * (quad % 2) + parity
                    for w in range(2):
                        at = (4 * quad + 2 * w + parity) * WT
                        for h in range(HEADS):
                            rows = slice(KD * h, KD * (h + 1))
                            last = nc.tensor.matmul(
                                psum[WT * w:WT * (w + 1), S_BANKS[part][h], tile * WT:(tile + 1) * WT],
                                qT[rows, at:at + WT], kT[rows, at:at + WT], start=True, stop=True)
                if quad % 2:
                    last.then_inc(scores_done, 1)

            def transpose_probs(u, h, buffer):
                pe.wait_ge(probs_ready, HEADS * u + h + 1)
                if h < 2:
                    pe.wait_ge(hT_copied, 2 * (u + 2) + h + 1)
                else:
                    pe.wait_ge(exp_done, 2 * HEADS * (u + 1) + 1)
                for quad in range(QUADS):
                    last = nc.tensor.transpose(
                        psum[:, PT_BANKS[h], quad * P:(quad + 1) * P],
                        probs[:, buffer, h, 2 * quad:2 * quad + 2, :].rearrange("p a k -> p (a k)"),
                        ident[:, :])
                last.then_inc(pt_done, 1)

            def score_and_transpose(u, buffer, first):
                pe.wait_ge(qk_copied, 4 * (u + 2))
                score(0)
                if not first:
                    project_out(u - 1, 1)
                score(1)
                transpose1(u + 2, 0, True)
                transpose1(u + 2, 1, True)
                if first:
                    wait_apart(pe, mlp_added, 2 * u + 1)
                else:
                    wait_apart(pe, attn_added, 2 * u)
                score(2)
                transpose_probs(u, 0, buffer)
                score(3)
                transpose_probs(u, 1, buffer)
                transpose_probs(u, 2, buffer)

            def attend(quad, buffer):
                for w in range(2):
                    at = (2 * quad + w) * WT
                    for parity in range(2):
                        keys = slice(WT * parity, WT * (parity + 1))
                        for h in range(HEADS):
                            last = nc.tensor.matmul(
                                psum[KD * h:KD * (h + 1), PV_BANKS[parity], at:at + WT],
                                v[keys, buffer, quad, w, KD * h:KD * (h + 1)],
                                probsT[keys, h, quad, WT * w:WT * (w + 1)], start=True, stop=True)
                if quad == QUADS - 1:
                    last.then_inc(pv_done, 1)

            def project_qk_and_attend(u, buffer):
                project_qk(u + 2, 0, True)
                project_qk(u + 2, 1, True)
                pe.wait_ge(pt_copied, HEADS * (u + 1))
                wait_apart(pe, exp_done, 2 * HEADS * (u + 1) + 2)
                attend(0, buffer)
                attend(1, buffer)
                project_qk(u + 2, 2, True)
                attend(2, buffer)
                attend(3, buffer)
                project_qk(u + 2, 3, True)

            def project_out(u, g):
                if g == 0:
                    pe.wait_ge(oT_copied, 2 * (u + 1))
                pe.wait_ge(exp_done, 2 * HEADS * (u + 1) + 5 + g)
                for t in range(TILES // 2):
                    c = g * (TILES // 2) + t
                    last = nc.tensor.matmul(psum[:, O_BANKS[g], t * C:(t + 1) * C],
                                            oT[:, c * P:(c + 1) * P], wo_w[:, :], start=True, stop=True)
                last.then_inc(o_done, 1)

            def attention_step(u, half, first):
                score_and_transpose(u, half, first)
                project_qk_and_attend(u, half)
                project_v(u + 2)
                project_out(u, 0)

            def transpose2(u, steady):
                pe.wait_ge(ln2_ready, u + 1)
                if steady:
                    pe.wait_ge(gelu_done, 2 * FCHUNKS * u - FCHUNKS)
                for g in range(2):
                    transpose_rows(normed2, T2_BANKS, g, t2_done)

            def up(u, part, steady):
                pe.wait_ge(h2T_copied, 2 * u + 1 + part)
                if part and steady:
                    pe.wait_ge(gelu_done, 2 * FCHUNKS * u)
                for j in range(FCHUNKS):
                    if part == 0 and j == 2:
                        pe.wait_ge(h2T_copied, 2 * u + 2)
                    for step, (w, h) in enumerate(SPLIT_STEPS):
                        last = nc.tensor.matmul(psum[:, UP_BANKS[part][j], :],
                                                w1_split[w][:, j * P:(j + 1) * P],
                                                h2T[h][:, part * SHARES:(part + 1) * SHARES],
                                                start=(step == 0), stop=(step == 2))
                    last.then_inc(up_done, 1)

            def down(u, part, steady):
                pe.wait_ge(gelu_done, 2 * FCHUNKS * u + FCHUNKS * (part + 1))
                if steady:
                    pe.wait_ge(mlp_added, 2 * u + part)
                for t in range(TILES // 2):
                    c = part * (TILES // 2) + t
                    for j in range(FCHUNKS):
                        last = nc.tensor.matmul(psum[:, DOWN_BANKS[part], t * C:(t + 1) * C],
                                                gelu[:, j, c * P:(c + 1) * P], w2_w[:, j, :],
                                                start=(j == 0), stop=(j == FCHUNKS - 1))
                last.then_inc(down_done, 1)

            def mlp_step(u, first, last):
                up(u, 1, not first)
                if not last:
                    transpose2(u + 1, True)
                down(u, 0, not first)
                if not last:
                    up(u + 1, 0, True)
                down(u, 1, not first)

            for g in range(2):
                transpose1(0, g, False)
            for n in range(4):
                project_qk(0, n, False)
            project_v(0)
            pe.wait_ge(qk_copied, 4)
            for quad in range(QUADS):
                score(quad)
            for g in range(2):
                transpose1(1, g, True)
            for n in range(4):
                project_qk(1, n, True)
            project_v(1)
            wait_apart(pe, exp_done, 2 * HEADS)

            with pe.Fori(0, BATCHES) as b:
                batch = b * BATCH
                attention_step(batch, 0, True)
                attention_step(batch + 1, 1, False)
                with pe.Fori(1, BATCH_ROWS) as r:
                    for half in (0, 1):
                        attention_step(batch + 2 * r + half, half, False)
                project_out(batch + BATCH - 1, 1)
                transpose2(batch, False)
                pe.wait_ge(exp_done, 2 * HEADS * (batch + BATCH + 1))
                pe.wait_ge(qk_copied, 4 * (batch + BATCH + 2))
                pe.wait_ge(v_copied, 2 * (batch + BATCH + 2))
                up(batch, 0, False)
                pe.wait_ge(attn_added, 2 * (batch + BATCH))
                mlp_step(batch, True, False)
                with pe.Fori(1, BATCH - 1) as j:
                    mlp_step(batch + j, False, False)
                mlp_step(batch + BATCH - 1, False, True)
                pe.wait_ge(gelu_done, 2 * FCHUNKS * (batch + BATCH))

        @block.scalar
        def _(act):
            def log1_of(u):
                act.wait_ge(ln1_step, LN_STEPS * (u + 1))
                nc.scalar.activation(log_var[0][:, :], sq_dev[0][:, :], ACT.Ln, bias=eps_col[:, :],
                                     scale=1.0 / C).then_inc(log1_step, 1)

            def rstd1_of(u):
                act.wait_ge(log1_step, u + 1)
                nc.scalar.activation(rstd1[:, :], log_var[0][:, :], ACT.Exp, scale=-0.5).then_inc(rstd1_ready, 1)

            def log2_of(u):
                act.wait_ge(ln2_step, LN_STEPS * (u + 1))
                nc.scalar.activation(log_var[1][:, :], sq_dev[1][:, :], ACT.Ln, bias=eps_col[:, :],
                                     scale=1.0 / C).then_inc(log2_step, 1)

            def rstd2_of(u):
                act.wait_ge(log2_step, u + 1)
                nc.scalar.activation(rstd2[:, u & (BATCH - 1), :], log_var[1][:, :], ACT.Exp, scale=-0.5)\
                    .then_inc(rstd2_ready, 1)

            def copy_hT_upper(u):
                ordered = hT_split[0][0:C, :].rearrange("c (w k r) -> c k w r", w=WINDOWS, r=4)
                for g in range(2):
                    act.wait_ge(t1_done, 2 * u + g + 1)
                    nc.scalar.activation(
                        ordered[:, 8 * g:8 * (g + 1), :, :],
                        psum[0:C, T_BANKS[g], :].rearrange("c (k w r) -> c k w r", k=8, r=4), ACT.Copy)\
                        .then_inc(hT_upper_copied, 1)

            def copy_qk(u, n):
                act.wait_ge(qk_done, 4 * u + n + 1)
                group, which = divmod(n, 2)
                nc.scalar.activation((qT, kT)[which][:, group * SHARES:(group + 1) * SHARES],
                                     psum[0:C, QK_BANKS[n], :], ACT.Copy).then_inc(qk_copied, 1)

            def copy_probsT(u, h):
                act.wait_ge(pt_done, HEADS * u + h + 1)
                nc.scalar.activation(probsT[:, h, :, :].rearrange("p q k -> p (q k)"),
                                     psum[:, PT_BANKS[h], :], ACT.Copy).then_inc(pt_copied, 1)

            def copy_v(u, buffer):
                for g in range(2):
                    act.wait_ge(v_done, 2 * u + g + 1)
                    nc.scalar.activation(v[:, buffer, 2 * g:2 * g + 2, :, :].rearrange("p q w c -> p (q w c)"),
                                         psum[:, V_BANKS[g], 0:GROUP], ACT.Copy).then_inc(v_copied, 1)

            def exps(u, buffer, part, h):
                act.wait_ge(bias_ready, 2 * u + part + 1)
                for t in range(PART):
                    tile = PART * part + t
                    last = nc.scalar.activation(
                        probs[:, buffer, h, tile, :],
                        psum[:, S_BANKS[part][h], t * WT:(t + 1) * WT], ACT.Exp,
                        bias=exp_bias[:, h, tile:tile + 1], scale=SCALE,
                        accum_out=prob_sum[:, h, tile:tile + 1])
                last.then_inc(exp_done, 1)

            def attention_step(u, half, first):
                other = 1 - half
                copy_hT_upper(u + 2)
                act.wait_ge(inv_ready, 2 * (u + 1))
                exps(u + 1, other, 0, 0)
                copy_probsT(u, 0)
                exps(u + 1, other, 0, 1)
                copy_probsT(u, 1)
                copy_probsT(u, 2)
                if not first:
                    log2_of(u - 1)
                exps(u + 1, other, 0, 2)
                if not first:
                    rstd2_of(u - 1)
                copy_qk(u + 2, 0)
                copy_qk(u + 2, 1)
                exps(u + 1, other, 1, 0)
                exps(u + 1, other, 1, 1)
                log1_of(u + 3)
                copy_qk(u + 2, 2)
                rstd1_of(u + 3)
                copy_qk(u + 2, 3)
                exps(u + 1, other, 1, 2)
                copy_v(u + 2, half)

            def gelus(u, part):
                for j in range(FCHUNKS):
                    act.wait_ge(up_done, 2 * FCHUNKS * u + FCHUNKS * part + j + 1)
                    nc.scalar.activation(gelu[:, j, part * SHARES:(part + 1) * SHARES],
                                         psum[:, UP_BANKS[part][j], :], ACT.Gelu).then_inc(gelu_done, 1)

            act.wait_ge(rows_cleared, 5)
            act.dma_start(wo_w[ONES:ONES + 1, :], bo.rearrange("(a n) -> a n", a=1)).then_inc(weights_in, 16)
            act.wait_ge(consts_set, 4)
            nc.scalar.preload_act_table_set("natural_log_exp_and_others")
            log1_of(0)
            rstd1_of(0)
            copy_hT_upper(0)
            for n in range(4):
                copy_qk(0, n)
            copy_v(0, 0)
            log1_of(1)
            rstd1_of(1)
            for part in range(2):
                for h in range(HEADS):
                    exps(0, 0, part, h)
            copy_hT_upper(1)
            for n in range(4):
                copy_qk(1, n)
            copy_v(1, 1)
            log1_of(2)
            rstd1_of(2)
            with act.Fori(0, BATCHES) as b:
                batch = b * BATCH
                nc.scalar.preload_act_table_set("natural_log_exp_and_others")
                attention_step(batch, 0, True)
                attention_step(batch + 1, 1, False)
                with act.Fori(1, BATCH_ROWS) as r:
                    for half in (0, 1):
                        attention_step(batch + 2 * r + half, half, False)
                log2_of(batch + BATCH - 1)
                rstd2_of(batch + BATCH - 1)
                nc.scalar.preload_act_table_set("gelu_and_others")
                with act.Fori(0, BATCH) as j:
                    gelus(batch + j, 0)
                    gelus(batch + j, 1)

        @block.vector
        def _(dve):
            nc.vector.memset(eps_col[:, :], EPS).then_inc(consts_set, 1)
            for rows in (qkv_w[C:P, :, :], wo_w[C:P, :], w1_w[C:P, :], hT[C:P, :], oT[C:P, :]):
                nc.vector.memset(rows, 0.0).then_inc(rows_cleared, 1)
            dve.wait_ge(rows_cleared, 5)
            for t in (hT, oT):
                nc.vector.memset(t[ONES:ONES + 1, :], 1.0).then_inc(consts_set, 1)
            dve.wait_ge(weights_in, 16 * (N_WEIGHT_DMAS + 1))
            nc.vector.tensor_scalar(qkv_w[0:C, :, :].rearrange("c i n -> c (i n)"),
                                    qkv_raw[:, :, :].rearrange("c i n -> c (i n)"),
                                    ln_cols[:, 0:1], None, ALU.mult).then_inc(weights_ready, 1)
            nc.vector.tensor_scalar(w1_w[0:C, :], w1_raw[:, :], ln_cols[:, 2:3], None, ALU.mult)\
                .then_inc(weights_ready, 1)
            dve.wait_ge(bias_folded, 1)
            dve.wait_ge(consts_set, 4)
            for upper, lower in (hT_split, h2T):
                nc.vector.tensor_copy(upper[C:P, :], oT[C:P, :])
                nc.vector.tensor_tensor(lower[C:P, :], oT[C:P, :], oT[C:P, :], ALU.subtract)
            nc.vector.tensor_tensor(qkv_w[ONES:ONES + 1, :, :].rearrange("c i n -> c (i n)"),
                                    psum[ONES:ONES + 1, 0, 0:3 * C], bias_rows[ONES:ONES + 1, 0:3 * C],
                                    ALU.add).then_inc(weights_ready, 1)
            nc.vector.tensor_tensor(w1_w[ONES:ONES + 1, :], psum[ONES:ONES + 1, 1, 0:F],
                                    bias_rows[ONES:ONES + 1, 3 * C:3 * C + F], ALU.add)\
                .then_inc(weights_ready, 1)
            dve.wait_ge(weights_ready, 4)
            split = ((w1_w[:, :], [half[:, :] for half in w1_split]),
                     (qkv_w[:, 0:2, :], [half[:, :, :] for half in qk_split]))
            for whole, (upper, lower) in split:
                nc.vector.tensor_copy(upper, whole).then_inc(split_step, 1)
            dve.wait_ge(split_step, 2)
            for whole, (upper, lower) in split:
                nc.vector.tensor_tensor(lower, whole, upper, ALU.subtract).then_inc(weights_ready, 1)

            def slot_of(u):
                return u % SLOTS if isinstance(u, int) else u & (SLOTS - 1)

            def statistics(u, i, step, mean):
                at = LN_STEPS * u
                slot = slot_of(u)
                for c in range(TILES):
                    last = nc.vector.bn_stats(stats[i][:, c, :], stream[:, slot, c * C:(c + 1) * C])
                last.then_inc(step, 1)
                dve.wait_ge(step, at + 1)
                even, odd = stats[i][:, :, 1], stats[i][:, :, 4]
                nc.vector.tensor_tensor(mean_gap[i][:, :], even, odd, ALU.subtract).then_inc(step, 1)
                nc.vector.tensor_tensor(within[i][:, :], stats[i][:, :, 2], stats[i][:, :, 5], ALU.add)
                nc.vector.tensor_tensor(mean_sum[i][:, :], even, odd, ALU.add).then_inc(step, 1)
                dve.wait_ge(step, at + 2)
                nc.vector.scalar_tensor_tensor(between[i][:, :], mean_gap[i][:, :], C / 4, mean_gap[i][:, :],
                                               ALU.mult, ALU.mult).then_inc(step, 1)
                dve.wait_ge(step, at + 3)
                nc.vector.tensor_scalar(mean, mean_sum[i][:, :], 0.5, None, ALU.mult).then_inc(step, 1)
                dve.wait_ge(step, at + 4)
                nc.vector.tensor_tensor(sq_dev[i][:, :], within[i][:, :], between[i][:, :], ALU.add)\
                    .then_inc(step, 1)

            def normalise(u, normed, mean, inv, ready):
                slot = slot_of(u)
                for c in range(TILES):
                    last = nc.vector.tensor_scalar(normed[:, c, :], stream[:, slot, c * C:(c + 1) * C],
                                                   mean[:, c:c + 1], inv[:, c:c + 1],
                                                   ALU.subtract, ALU.mult)
                last.then_inc(ready, 1)

            def statistics1(u, row, half):
                wait_apart(dve, x_loaded[half], 16 * LOAD_DMAS[half] * (row + 1))
                statistics(u, 0, ln1_step, mean1[:, :])

            def normalise1(u):
                dve.wait_ge(rstd1_ready, u + 1)
                normalise(u, normed1, mean1, rstd1, ln1_ready)

            def copy_hT_lower(u, g):
                upper, lower = [half[0:C, :].rearrange("c (w k r) -> c k w r", w=WINDOWS, r=4)
                                for half in hT_split]
                dve.wait_ge(hT_upper_copied, 2 * u + g + 1)
                rows = slice(8 * g, 8 * (g + 1))
                nc.vector.tensor_tensor(
                    lower[:, rows, :, :],
                    psum[0:C, T_BANKS[g], :].rearrange("c (k w r) -> c k w r", k=8, r=4),
                    upper[:, rows, :, :], ALU.subtract).then_inc(hT_copied, 1)

            def maxima(u, part):
                dve.wait_ge(scores_done, 2 * u + part + 1)
                tiles = slice(PART * part, PART * (part + 1))
                first = S_BANKS[part][0]
                nc.vector.tensor_reduce(
                    neg_max[:, :, tiles],
                    psum[:, first:first + HEADS, 0:PART * WT].rearrange("p h (t k) -> p h t k", k=WT),
                    AXIS.X, ALU.max, negate=True).then_inc(max_step, 1)
                dve.wait_ge(max_step, 2 * u + part + 1)
                nc.vector.tensor_scalar(exp_bias[:, :, tiles], neg_max[:, :, tiles], SCALE, None, ALU.mult)\
                    .then_inc(bias_ready, 1)

            def invert_sums(u, first, last, steady):
                dve.wait_ge(exp_done, 2 * HEADS * u + HEADS + last)
                if steady and first == 0:
                    dve.wait_ge(probs_ready, HEADS * u)
                nc.vector.reciprocal(
                    prob_inv[:, first:last, :].rearrange("p h t -> p (h t)"),
                    prob_sum[:, first:last, :].rearrange("p h t -> p (h t)")).then_inc(inv_ready, 1)

            def copy_oT(u):
                dve.wait_ge(pv_done, u + 1)
                ordered = oT[0:C, :].rearrange("c (k n a r) -> c a n k r", k=16, a=2, r=4)
                for parity in range(2):
                    nc.vector.tensor_copy(
                        ordered[:, parity, :, :, :],
                        psum[0:C, PV_BANKS[parity], :].rearrange("c (n k r) -> c n k r", k=16, r=4))\
                        .then_inc(oT_copied, 1)

            def add_into_stream(u, banks, g, added):
                part = stream[:, slot_of(u), g * GROUP:(g + 1) * GROUP]
                nc.vector.tensor_tensor(part, part, psum[:, banks[g], 0:GROUP], ALU.add).then_inc(added, 1)

            def add_attention(u, g):
                dve.wait_ge(o_done, 2 * u + g + 1)
                add_into_stream(u, O_BANKS, g, attn_added)

            def statistics2(u):
                wait_apart(dve, attn_added, 2 * (u + 1))
                statistics(u, 1, ln2_step, mean2[:, u & (BATCH - 1), :])

            def normalise2(b, j):
                u = b * BATCH + j
                dve.wait_ge(rstd2_ready, u + 1)
                nc.vector.tensor_copy(mean2_now[:, :], mean2[:, u & (BATCH - 1), :]).then_inc(copy_step, 1)
                nc.vector.tensor_copy(rstd2_now[:, :], rstd2[:, u & (BATCH - 1), :]).then_inc(copy_step, 1)
                dve.wait_ge(copy_step, 2 * ((BATCH - 1) * b + j))
                normalise(u, normed2, mean2_now, rstd2_now, ln2_ready)

            def copy_h2T(u):
                tokens = [slice(g * SHARES, (g + 1) * SHARES) for g in range(2)]
                for g in range(2):
                    dve.wait_ge(t2_done, 2 * u + g + 1)
                    nc.vector.tensor_copy(h2T[0][0:C, tokens[g]], psum[0:C, T2_BANKS[g], :])\
                        .then_inc(upper_step, 1)
                for g in range(2):
                    dve.wait_ge(upper_step, 2 * u + g + 1)
                    nc.vector.tensor_tensor(h2T[1][0:C, tokens[g]], psum[0:C, T2_BANKS[g], :],
                                            h2T[0][0:C, tokens[g]], ALU.subtract).then_inc(h2T_copied, 1)

            def add_mlp(u):
                dve.wait_ge(b2_added, u + 1)
                for g in range(2):
                    dve.wait_ge(down_done, 2 * u + g + 1)
                    add_into_stream(u, DOWN_BANKS, g, mlp_added)

            dve.sem_inc(mlp_added, 1)
            statistics1(0, 0, 0)
            normalise1(0)
            for g in range(2):
                copy_hT_lower(0, g)
            statistics1(1, 0, 1)
            normalise1(1)
            for part in range(2):
                maxima(0, part)
            for g in range(2):
                copy_hT_lower(1, g)
            statistics1(2, 1, 0)
            normalise1(2)
            invert_sums(0, 0, 2, False)
            invert_sums(0, 2, 3, False)

            def attention_step(row, half, first):
                u = 2 * row + half
                if not first:
                    add_attention(u - 1, 1)
                maxima(u + 1, 0)
                copy_hT_lower(u + 2, 0)
                copy_hT_lower(u + 2, 1)
                if not first:
                    statistics2(u - 1)
                maxima(u + 1, 1)
                statistics1(u + 3, row + 1 + half, 1 - half)
                copy_oT(u)
                invert_sums(u + 1, 0, 2, True)
                normalise1(u + 3)
                invert_sums(u + 1, 2, 3, True)
                add_attention(u, 0)

            with dve.Fori(0, BATCHES) as b:
                batch_row = b * BATCH_ROWS
                attention_step(batch_row, 0, True)
                attention_step(batch_row, 1, False)
                batch = 2 * batch_row
                with dve.Fori(1, BATCH_ROWS) as r:
                    for half in (0, 1):
                        attention_step(batch_row + r, half, False)
                add_attention(batch + BATCH - 1, 1)
                copy_h2T(batch)
                statistics2(batch + BATCH - 1)
                normalise2(b, 1)
                with dve.Fori(0, BATCH - 2) as j:
                    copy_h2T(batch + j + 1)
                    normalise2(b, j + 2)
                    add_mlp(batch + j)
                copy_h2T(batch + BATCH - 1)
                add_mlp(batch + BATCH - 2)
                add_mlp(batch + BATCH - 1)


_INS = ["x", "L0_conv_ln1_g", "L0_conv_ln1_b", "L0_conv_wq", "L0_conv_bq", "L0_conv_wk", "L0_conv_bk",
        "L0_conv_wv", "L0_conv_bv", "L0_conv_wo", "L0_conv_bo", "L0_conv_ln2_g", "L0_conv_ln2_b",
        "L0_conv_w1", "L0_conv_b1", "L0_conv_w2", "L0_conv_b2"]


def kernel(**inputs):
    import numpy as np
    import concourse.bacc as bacc
    from concourse.bass_utils import run_bass_kernel_spmd

    nc = bacc.Bacc("TRN2", target_bir_lowering=False, num_devices=1)
    arrays, args = {}, []
    for name in _INS:
        a = np.ascontiguousarray(inputs[name])
        arrays[f"in_{name}"] = a
        args.append(nc.dram_tensor(f"in_{name}", a.shape, mybir.dt.from_np(a.dtype), kind="ExternalInput").ap())
    out = nc.dram_tensor("out", (IMAGES, HEIGHT, WIDTH, C), FP32, kind="ExternalOutput").ap()
    swin_block(nc, *args, out)
    result = run_bass_kernel_spmd(nc, [arrays], core_ids=[0])
    return result.results[0]["out"]
```
